# Optimizing a Trainium2 kernel written in Bass

```python
import numpy as np
import jax
import jax.numpy as jnp

def _softmax(x, axis=-1):
    return jax.nn.softmax(x, axis=axis)

def _gelu(x):
    return jax.nn.gelu(x, approximate=True)

def _silu(x):
    return jax.nn.silu(x)

def _sigmoid(x):
    return jax.nn.sigmoid(x)

def _layernorm(x, axis=-1, eps=1e-05):
    m = jnp.mean(x, axis=axis, keepdims=True)
    v = jnp.var(x, axis=axis, keepdims=True)
    return (x - m) / jnp.sqrt(v + eps)

def _scatter_add(tgt, idx, src, axis=0):
    return tgt.at[idx].add(src)

def _segment_sum(src, seg, n):
    return jax.ops.segment_sum(src, seg, n)
kernel_name = 'mk_seq_postln_d1_jaxref_r4_a83b12'

def setup_inputs(seed: int=0):
    np.random.seed(seed)
    _w = jnp.asarray

    def _L0_attn_setup():
        import jax, jax.numpy as jnp
        import numpy as np
        LN_EPS = 1e-05

        def _layernorm(x, g, b):
            mu = jnp.mean(x, axis=-1, keepdims=True)
            var = jnp.var(x, axis=-1, keepdims=True)
            return (x - mu) * jax.lax.rsqrt(var + LN_EPS) * g + b
        key = jax.random.key(seed)
        B, S, D, H = (2, 512, 256, 16)
        dh = D // H
        r = 48
        r_out = 192
        I = 4 * D
        r_mlp = 128
        ks = jax.random.split(key, 24)
        sc = lambda *sh: 0.02
        inp = {'hidden_states': jax.random.normal(ks[0], (B, S, D), jnp.float32), 'ln1_g': jnp.ones((D,), jnp.float32), 'ln1_b': jnp.zeros((D,), jnp.float32), 'ln2_g': jnp.ones((D,), jnp.float32), 'ln2_b': jnp.zeros((D,), jnp.float32), 'q_U': jax.random.normal(ks[1], (D, H, r), jnp.float32) * 0.02, 'q_V': jax.random.normal(ks[2], (H, r, dh), jnp.float32) * 0.02, 'q_b': jax.random.normal(ks[3], (H, dh), jnp.float32) * 0.02, 'k_U': jax.random.normal(ks[4], (D, H, r), jnp.float32) * 0.02, 'k_V': jax.random.normal(ks[5], (H, r, dh), jnp.float32) * 0.02, 'k_b': jax.random.normal(ks[6], (H, dh), jnp.float32) * 0.02, 'v_U': jax.random.normal(ks[7], (D, H, r), jnp.float32) * 0.02, 'v_V': jax.random.normal(ks[8], (H, r, dh), jnp.float32) * 0.02, 'v_b': jax.random.normal(ks[9], (H, dh), jnp.float32) * 0.02, 'out_U': jax.random.normal(ks[10], (D, r_out), jnp.float32) * 0.02, 'out_V': jax.random.normal(ks[11], (r_out, D), jnp.float32) * 0.02, 'out_b': jnp.zeros((D,), jnp.float32), 'fc1_U': jax.random.normal(ks[12], (D, r_mlp), jnp.float32) * 0.02, 'fc1_V': jax.random.normal(ks[13], (r_mlp, I), jnp.float32) * 0.02, 'fc1_b': jnp.zeros((I,), jnp.float32), 'fc2_U': jax.random.normal(ks[14], (I, r_mlp), jnp.float32) * 0.02, 'fc2_V': jax.random.normal(ks[15], (r_mlp, D), jnp.float32) * 0.02, 'fc2_b': jnp.zeros((D,), jnp.float32)}
        return inp
    _L0_attn_in = _L0_attn_setup()

    def _L0_ffn_setup():
        import jax, jax.numpy as jnp
        import numpy as np
        FEATURES = 256
        D_IN = 256

        def fp8_gemm_optimized(x, input_scale, kernel, kernel_scale):
            s_in = input_scale[0]
            s_k = kernel_scale[0]
            x_q = (x.astype(jnp.float32) / s_in).astype(jnp.float8_e4m3fn)
            k_q = (kernel.astype(jnp.float32) / s_k).astype(jnp.float8_e4m3fn)
            y = jnp.dot(x_q.astype(jnp.float32), k_q.astype(jnp.float32), preferred_element_type=jnp.float32)
            return y * (s_in * s_k)
        key = jax.random.key(seed)
        kx, kk, kb = jax.random.split(key, 3)
        x = jax.random.normal(kx, (4, 2048, D_IN), dtype=jnp.float32)
        limit = np.sqrt(6.0 / (D_IN + FEATURES)).astype(np.float32)
        kernel = jax.random.uniform(kk, (D_IN, FEATURES), dtype=jnp.float32, minval=-limit, maxval=limit).astype(jnp.bfloat16)
        input_scale = jnp.ones((1,), dtype=jnp.float32)
        kernel_scale = jnp.ones((1,), dtype=jnp.float32)
        bias = jnp.zeros((FEATURES,), dtype=jnp.bfloat16)
        return {'x': x, 'kernel': kernel, 'input_scale': input_scale, 'kernel_scale': kernel_scale, 'bias': bias}
    _L0_ffn_in = _L0_ffn_setup()
    _d = {'L0_attn_hidden_states': _L0_attn_in['hidden_states'], 'L0_attn_ln1_g': _L0_attn_in['ln1_g'], 'L0_attn_ln1_b': _L0_attn_in['ln1_b'], 'L0_attn_ln2_g': _L0_attn_in['ln2_g'], 'L0_attn_ln2_b': _L0_attn_in['ln2_b'], 'L0_attn_q_U': _L0_attn_in['q_U'], 'L0_attn_q_V': _L0_attn_in['q_V'], 'L0_attn_q_b': _L0_attn_in['q_b'], 'L0_attn_k_U': _L0_attn_in['k_U'], 'L0_attn_k_V': _L0_attn_in['k_V'], 'L0_attn_k_b': _L0_attn_in['k_b'], 'L0_attn_v_U': _L0_attn_in['v_U'], 'L0_attn_v_V': _L0_attn_in['v_V'], 'L0_attn_v_b': _L0_attn_in['v_b'], 'L0_attn_out_U': _L0_attn_in['out_U'], 'L0_attn_out_V': _L0_attn_in['out_V'], 'L0_attn_out_b': _L0_attn_in['out_b'], 'L0_attn_fc1_U': _L0_attn_in['fc1_U'], 'L0_attn_fc1_V': _L0_attn_in['fc1_V'], 'L0_attn_fc1_b': _L0_attn_in['fc1_b'], 'L0_attn_fc2_U': _L0_attn_in['fc2_U'], 'L0_attn_fc2_V': _L0_attn_in['fc2_V'], 'L0_attn_fc2_b': _L0_attn_in['fc2_b'], 'L0_ffn_kernel': _L0_ffn_in['kernel'], 'L0_ffn_input_scale': _L0_ffn_in['input_scale'], 'L0_ffn_kernel_scale': _L0_ffn_in['kernel_scale'], 'L0_ffn_bias': _L0_ffn_in['bias']}
    _x0 = _d['L0_attn_hidden_states']
    _d['L0_attn_hidden_states'] = jax.random.normal(jax.random.fold_in(jax.random.key(seed), 1), (8, 1024, 256), dtype=_x0.dtype)
    del _x0
    return _d

def reference(L0_attn_hidden_states, L0_attn_ln1_g, L0_attn_ln1_b, L0_attn_ln2_g, L0_attn_ln2_b, L0_attn_q_U, L0_attn_q_V, L0_attn_q_b, L0_attn_k_U, L0_attn_k_V, L0_attn_k_b, L0_attn_v_U, L0_attn_v_V, L0_attn_v_b, L0_attn_out_U, L0_attn_out_V, L0_attn_out_b, L0_attn_fc1_U, L0_attn_fc1_V, L0_attn_fc1_b, L0_attn_fc2_U, L0_attn_fc2_V, L0_attn_fc2_b, L0_ffn_kernel, L0_ffn_input_scale, L0_ffn_kernel_scale, L0_ffn_bias):

    def _L0_attn_ref(hidden_states, ln1_g, ln1_b, ln2_g, ln2_b, q_U, q_V, q_b, k_U, k_V, k_b, v_U, v_V, v_b, out_U, out_V, out_b, fc1_U, fc1_V, fc1_b, fc2_U, fc2_V, fc2_b):
        import jax, jax.numpy as jnp
        import numpy as np
        LN_EPS = 1e-05

        def _layernorm(x, g, b):
            mu = jnp.mean(x, axis=-1, keepdims=True)
            var = jnp.var(x, axis=-1, keepdims=True)
            return (x - mu) * jax.lax.rsqrt(var + LN_EPS) * g + b
        B, S, D = hidden_states.shape
        H, dh = (q_V.shape[0], q_V.shape[2])
        x = _layernorm(hidden_states, ln1_g, ln1_b)
        Q = jnp.einsum('bsd,dhr,hre->bhse', x, q_U, q_V) + q_b[None, :, None, :]
        Pk = jnp.einsum('bsd,dhr->bhsr', x, k_U)
        Pv = jnp.einsum('bsd,dhr->bhsr', x, v_U)
        K = jnp.einsum('bhsr,hrd->bhsd', Pk, k_V) + k_b[None, :, None, :]
        V = jnp.einsum('bhsr,hrd->bhsd', Pv, v_V) + v_b[None, :, None, :]
        scale = 1.0 / jnp.sqrt(jnp.asarray(dh, x.dtype))
        scores = jnp.einsum('bhse,bhte->bhst', Q, K) * scale
        causal = jnp.tril(jnp.ones((S, S), bool))
        scores = jnp.where(causal[None, None], scores, jnp.asarray(-1000000000.0, scores.dtype))
        attn = jax.nn.softmax(scores, axis=-1)
        ctx = jnp.einsum('bhst,bhtd->bhsd', attn, V)
        ctx = ctx.transpose(0, 2, 1, 3).reshape(B, S, D)
        attn_out = ctx @ out_U @ out_V + out_b
        h = hidden_states + attn_out
        x2 = _layernorm(h, ln2_g, ln2_b)
        hmid = jax.nn.gelu(x2 @ fc1_U @ fc1_V + fc1_b, approximate=True)
        mlp_out = hmid @ fc2_U @ fc2_V + fc2_b
        return h + mlp_out

    def _L0_ffn_ref(x, kernel, input_scale, kernel_scale, bias):
        import jax, jax.numpy as jnp
        import numpy as np
        FEATURES = 256
        D_IN = 256

        def fp8_gemm_optimized(x, input_scale, kernel, kernel_scale):
            s_in = input_scale[0]
            s_k = kernel_scale[0]
            x_q = (x.astype(jnp.float32) / s_in).astype(jnp.float8_e4m3fn)
            k_q = (kernel.astype(jnp.float32) / s_k).astype(jnp.float8_e4m3fn)
            y = jnp.dot(x_q.astype(jnp.float32), k_q.astype(jnp.float32), preferred_element_type=jnp.float32)
            return y * (s_in * s_k)
        dtype = jnp.bfloat16
        x = x.astype(dtype)
        orig_shape = x.shape
        x2 = x.reshape(-1, x.shape[-1])
        y = fp8_gemm_optimized(x2, input_scale, kernel, kernel_scale)
        y = y.astype(dtype) + bias
        return y.reshape(orig_shape[:-1] + (FEATURES,))
    x = L0_attn_hidden_states
    x = _layernorm(x + _L0_attn_ref(x, L0_attn_ln1_g, L0_attn_ln1_b, L0_attn_ln2_g, L0_attn_ln2_b, L0_attn_q_U, L0_attn_q_V, L0_attn_q_b, L0_attn_k_U, L0_attn_k_V, L0_attn_k_b, L0_attn_v_U, L0_attn_v_V, L0_attn_v_b, L0_attn_out_U, L0_attn_out_V, L0_attn_out_b, L0_attn_fc1_U, L0_attn_fc1_V, L0_attn_fc1_b, L0_attn_fc2_U, L0_attn_fc2_V, L0_attn_fc2_b), axis=-1)
    x = _layernorm(x + _L0_ffn_ref(x, L0_ffn_kernel, L0_ffn_input_scale, L0_ffn_kernel_scale, L0_ffn_bias), axis=-1)
    return x

_drawn_inputs = setup_inputs


def setup_inputs(seed=0):
    import zlib

    import numpy as np

    out = dict(_drawn_inputs(seed))
    spreads = {'L0_attn_ln1_g': (1.0, 0.6),
     'L0_attn_ln1_b': (0.0, 0.8),
     'L0_attn_ln2_g': (1.0, 0.6),
     'L0_attn_ln2_b': (0.0, 0.8),
     'L0_attn_out_b': (0.0, 0.8),
     'L0_attn_fc1_b': (0.0, 0.8),
     'L0_attn_fc2_b': (0.0, 0.8),
     'L0_ffn_bias': (0.0, 0.1)}
    factors = {'L0_attn_q_U': 8.0,
     'L0_attn_q_V': 8.0,
     'L0_attn_q_b': 8.0,
     'L0_attn_k_U': 8.0,
     'L0_attn_k_V': 8.0,
     'L0_attn_k_b': 64.0,
     'L0_attn_v_U': 8.0,
     'L0_attn_v_V': 8.0,
     'L0_attn_v_b': 8.0,
     'L0_attn_out_U': 8.0,
     'L0_attn_out_V': 8.0,
     'L0_attn_fc1_U': 7.202,
     'L0_attn_fc1_V': 7.2,
     'L0_attn_fc2_U': 5.68,
     'L0_attn_fc2_V': 5.912}
    for name, (base, spread) in spreads.items():
        noise = np.random.default_rng([zlib.crc32(name.encode()), seed]).standard_normal(out[name].shape)
        drawn = base * np.exp(spread * noise) if base else spread * noise
        out[name] = jnp.asarray(drawn.astype(out[name].dtype))
    for name, factor in factors.items():
        out[name] = (out[name] * factor).astype(out[name].dtype)
    return out
```

```python
from contextlib import ExitStack

import numpy as np

import concourse.bass as bass
from concourse import mybir

ALU = mybir.AluOpType
ACT = mybir.ActivationFunctionType
AX = mybir.AxisListType
F32 = mybir.dt.float32
BF16 = mybir.dt.bfloat16
U32 = mybir.dt.uint32

P = 128
B, S, D = 8, 1024, 256
H, DH, R = 16, 16, 48
R_OUT, R_MLP, FF = 192, 128, 1024
T = S // P
C = D // P
HALF = S // 2
TH = T // 2
F = FF // P
G = 4
HG = H // G
SPLIT = 6
KS = SPLIT * DH
MROWS = 3
KM = KS + MROWS
Q_PARTS = (0, 0, 0, 1, 1, 2)
K_PARTS = (0, 1, 2, 0, 1, 0)
EPS = 1e-5
NEG = -1.0e30
SCALE = DH ** -0.5

STEPS = [(c, j) for c in range(2) for j in range(TH * (c + 1))]
NST = len(STEPS)
UNITS = [(hh, i, part) for hh in range(HG) for i in range(T) for part in range(1 + (i >= TH))]
NU = len(UNITS)
PER_STEP = NU // NST
A_RING, S_RING, NPT, TRASH = 2, 3, 2, 2
DIAG = [n for n, (c, j) in enumerate(STEPS) if j >= TH * c]


def schedule():
    more = {n: [] for n in range(G * NST)}

    def at(n, db, stage, *args):
        more[n].append((db, stage, args))

    at(0, 0, "place", 3)
    at(0, 0, "max_rows", 1)
    at(0, 1, "load_x", 0)
    at(1, 0, "v", 3)
    at(1, 1, "ln1_stats", 0)
    at(2, 1, "ln1_apply", 0)
    at(2, -1, "load_res", 0)
    for ch in range(C):
        at(3, -1, "ctx_t", 0, ch)
        at(4, 1, "x1_t", 0, ch)
    at(4, 1, "load_x", 1)
    for pr in range(2):
        at(5, -1, "out_proj", 0, pr)
    at(5, 1, "ln1_stats", 1)
    for ch in range(C):
        at(6, -1, "ctx_t", 1, ch)
    at(6, 1, "ln1_apply", 1)
    at(6, -1, "ln2_stats", 0)
    at(7, -1, "ln2_apply", 0)
    for ch in range(C):
        at(7, 1, "x1_t", 1, ch)
        at(8, -1, "x2_t", 0, ch)
    for n in range(4):
        at(8 + n, 1, "qk", n)
    at(9, -1, "fc1_u", 0)
    for f in range(F):
        at(10 + f // 2, -1, "fc1_v", 0, f)
    at(12, 1, "place", 0)
    at(12, 0, "max_rows", 2)
    at(13, -1, "gelu", 0)
    at(14, 1, "v", 0)
    at(15, -1, "fc2_u", 0)
    for pr in range(2):
        at(16, -1, "fc2_v", 0, pr)
    at(17, -1, "ln3_stats", 0)
    at(18, -1, "ln3_apply", 0)
    at(19, -1, "quant", 0)
    for ch in range(C):
        at(21, -1, "zq_t", 0, ch)
    for pr in range(2):
        at(22, -1, "ffn", 0, pr)
    at(23, -1, "ln4_stats", 0)
    at(24, -1, "ln4_apply", 0)
    at(24, -1, "store", 0)
    at(24, -1, "load_res", 1)
    at(24, 1, "place", 1)
    at(24, 0, "max_rows", 3)
    for pr in range(2):
        at(27, -1, "out_proj", 1, pr)
    at(28, -1, "ln2_stats", 1)
    at(29, -1, "ln2_apply", 1)
    for n in range(4):
        at(29 + n, 1, "qk", 4 + n)
    for ch in range(C):
        at(30, -1, "x2_t", 1, ch)
    at(31, -1, "fc1_u", 1)
    for f in range(F):
        at(32 + f // 2, -1, "fc1_v", 1, f)
    at(35, -1, "gelu", 1)
    at(36, 1, "place", 2)
    at(36, 1, "max_rows", 0)
    at(38, -1, "fc2_u", 1)
    for pr in range(2):
        at(39, -1, "fc2_v", 1, pr)
    at(40, -1, "ln3_stats", 1)
    at(41, -1, "ln3_apply", 1)
    at(42, -1, "quant", 1)
    for ch in range(C):
        at(44, -1, "zq_t", 1, ch)
    for pr in range(2):
        at(45, -1, "ffn", 1, pr)
    at(46, -1, "ln4_stats", 1)
    at(46, 1, "v", 1)
    at(47, 1, "v", 2)
    at(47, -1, "ln4_apply", 1)
    at(47, -1, "store", 1)

    out = []
    for n in range(G * NST):
        g, st = divmod(n, NST)
        a = (0, g + 2) if g < 2 else (1, g - 2)
        for hh in range(HG):
            out.append((0, "scores", (g, st, hh)))
            for u in range(st * PER_STEP + hh * PER_STEP // HG, st * PER_STEP + (hh + 1) * PER_STEP // HG):
                out.append((a[0], "row_max", (a[1], u)))
        db, m = (0, n - 1) if n else (-1, G * NST - 1)
        out.append((db, "values", divmod(m, NST)))
        if STEPS[m % NST][1] == TH * (STEPS[m % NST][0] + 1) - 1:
            out.append((db, "out_copy", (m // NST, STEPS[m % NST][0])))
        out += more[n]
        if STEPS[m % NST][1] == TH * (STEPS[m % NST][0] + 1) - 1:
            out.append((db, "out_norm", (m // NST, STEPS[m % NST][0])))
        if st == NST - 1:
            out.append((a[0], "max_parts", (a[1],)))
    return out


def build(nc, hidden, ln1_g, ln1_b, ln2_g, ln2_b, q_U, q_V, q_b, k_U, k_V, k_b, v_U, v_V, v_b,
          out_U, out_V, out_b, fc1_U, fc1_V, fc1_b, fc2_U, fc2_V, fc2_b, ffn_w, in_scale, w_scale,
          ffn_bias, out):
    SCHED = schedule()
    with ExitStack() as ctx:
        def sb(name, shape, dt=F32):
            return ctx.enter_context(nc.sbuf_tensor(name, shape, dt))

        def sem(name):
            return ctx.enter_context(nc.semaphore(name))

        slots = sb("slots", [P, G, HG, 2, S], BF16)
        qs, ks = slots[:, :, :, 0, :], slots[:, :, :, 1, :]
        vs = sb("vs", [P, T, H, DH + 1])
        probs = sb("probs", [P, NPT, HG, HALF])
        parts = sb("parts", [P, 2, 3, S], BF16)
        qk_full = sb("qk_full", [P, HALF])
        qk_rest = sb("qk_rest", [P, HALF])
        x_in = sb("x_in", [P, TH, D])
        x1t = sb("x1t", [P, C, S])
        ctx_sb = sb("ctx_sb", [P, T, D])
        ctx_t = sb("ctx_t", [P, 2, C, HALF])
        o_sb = sb("o_sb", [P, HALF])
        x_res = sb("x_res", [P, TH, D])
        h_sb = sb("h_sb", [P, TH, D])
        x2 = sb("x2", [P, TH, D])
        x2t = sb("x2t", [P, C, HALF])
        u_t = sb("u_t", [P, HALF])
        hid = sb("hid", [P, F, HALF])
        w_t = sb("w_t", [P, HALF])
        zq = sb("zq", [P, TH, D], BF16)
        zqt = sb("zqt", [P, C, HALF], BF16)
        yb = sb("yb", [P, TH, D], BF16)
        trash = sb("trash", [P, TRASH, HALF], BF16)
        m_rows = sb("m_rows", [MROWS * HG, S], BF16)
        mx = sb("mx", [P, T, HG])
        mx_hi = sb("mx_hi", [P, TH, HG])
        m_part = sb("m_part", [P, T, HG, MROWS], BF16)
        m_rest = sb("m_rest", [P, T, HG])
        rden = sb("rden", [P, TH, HG, 1])
        LN = range(1, 5)
        st6 = {n: sb(f"st6_{n}", [P, TH, 6]) for n in LN}
        mv = {n: sb(f"mv_{n}", [P, TH, 2]) for n in LN}
        var_eps = {n: sb(f"var_eps_{n}", [P, TH]) for n in LN}
        rstd = {n: sb(f"rstd_{n}", [P, TH]) for n in LN}
        wq = sb("wq", [P, C, D])
        wk = sb("wk", [P, C, D])
        wv = sb("wv", [P, C, D])
        wo = sb("wo", [P, C, D])
        w1u = sb("w1u", [P, C, R_MLP])
        w1v = sb("w1v", [P, FF])
        w2u = sb("w2u", [P, F, R_MLP])
        w2v = sb("w2v", [P, D])
        wf = sb("wf", [P, C, D], BF16)
        vb = sb("vb", [P, D])
        ob = sb("ob", [P, D])
        b2 = sb("b2", [P, D])
        fb = sb("fb", [P, D], BF16)
        g1 = sb("g1", [P, C])
        b1 = sb("b1", [P, C])
        g2 = sb("g2", [P, C])
        bb2 = sb("bb2", [P, C])
        qb = sb("qb", [P, 2])
        kb = sb("kb", [P, 2])
        fc1b = sb("fc1b", [P, F])
        sc = sb("sc", [P, 5])
        ident = sb("ident", [P, P])
        ident_b = sb("ident_b", [P, P], BF16)
        mask = sb("mask", [P, HALF])
        mask_t = sb("mask_t", [P, P], BF16)
        half_neg = sb("half_neg", [P, TH])

        bank = [ctx.enter_context(nc.psum_tensor(f"bank{n}", [P, HALF], F32)) for n in range(8)]
        pa, ps, po, px = bank[0:2], bank[2:5], bank[5], bank[6:8]

        names_in = ["q_in", "k_in", "v_in", "out_in", "rest_in"]
        loaded = {n: sem(n) for n in names_in}
        ident_ok, mask_ok, ones_ok = sem("ident_ok"), sem("mask_ok"), sem("ones_ok")
        ut_pe, ut_sb, fold_pe, fold_sb = sem("ut_pe"), sem("ut_sb"), sem("fold_pe"), sem("fold_sb")
        scale_ok, wf_ok = sem("scale_ok"), sem("wf_ok")
        x_loaded = sem("x_loaded")
        ln = {n: {k: sem(f"ln{n}_{k}") for k in ("stats", "aggr", "var", "rstd", "norm")} for n in LN}
        x1t_pe, x1t_sb = sem("x1t_pe"), sem("x1t_sb")
        qk_pe, qk_hi, qk_x, qk_r, qk_mid, qk_lo = (sem(n) for n in ("qk_pe", "qk_hi", "qk_x", "qk_r", "qk_mid", "qk_lo"))
        placed = [sem(f"placed{g}") for g in range(G)]
        v_pe, v_sb = sem("v_pe"), sem("v_sb")
        max_scores, row_max, neg_max = sem("max_scores"), sem("row_max"), sem("neg_max")
        mt_pe, mt_sb, m_placed = sem("mt_pe"), sem("mt_sb"), sem("m_placed")
        scores_pe, exp_done, pv_pe = sem("scores_pe"), sem("exp_done"), sem("pv_pe")
        o_copied, o_t, o_rden, ctx_ok = sem("o_copied"), sem("o_t"), sem("o_rden"), sem("ctx_ok")
        res_loaded, res_ob, res_b2, res_h = sem("res_loaded"), sem("res_ob"), sem("res_b2"), sem("res_h")
        ct_pe, ct_sb, op_pe, h_ok = sem("ct_pe"), sem("ct_sb"), sem("op_pe"), sem("h_ok")
        x2t_pe, x2t_sb, u_pe, u_sb = sem("x2t_pe"), sem("x2t_sb"), sem("u_pe"), sem("u_sb")
        hid_pe, hid_raw, hid_ok = sem("hid_pe"), sem("hid_raw"), sem("hid_ok")
        w_pe, w_sb, y_pe, y_ok = sem("w_pe"), sem("w_sb"), sem("y_pe"), sem("y_ok")
        quant_v, quant_p = sem("quant_v"), sem("quant_p")
        zt_pe, zt_sb, ffn_pe, ffn_y, ffn_b, ffn_sum = (sem(n) for n in ("zt_pe", "zt_sb", "ffn_pe", "ffn_y", "ffn_b", "ffn_sum"))
        stored = sem("stored")

        raw, tr = (slots[:, 2 * n:2 * n + 2, :, :, :].rearrange("p g h w s -> p (g h w s)").bitcast(F32) for n in range(2))
        u_raw = [raw[:, n * 1536:(n + 1) * 1536].rearrange("p (c x) -> p c x", c=C) for n in range(3)]
        v_raw = [raw[0:R, 4608 + n * D:4608 + (n + 1) * D] for n in range(3)]
        ou_raw = raw[:, 5376:5760].rearrange("p (c x) -> p c x", c=C)
        ov_raw = [raw[:, 5760:6016], raw[0:R_OUT - P, 6016:6272]]
        wf_raw = raw[:, 6272:6528].bitcast(BF16).rearrange("p (c n) -> p c n", c=C)
        ut = tr[0:R, 0:4096].rearrange("p (h c d) -> p h c d", h=H, c=C)
        out_t = [tr[:, 4096:4352], tr[0:R_OUT - P, 4352:4608]]
        q_v = hid[:, 0:2, :].rearrange("p a b -> p (a b)")
        q_m = hid[:, 2:4, :].rearrange("p a b -> p (a b)")
        q_t = hid[:, 4:6, :].rearrange("p a b -> p (a b)")
        q_n = hid[:, 6:8, :].rearrange("p a b -> p (a b)")

        flat = "p a b -> p (a b)"

        def need_first(eng, *events):
            values = [n if isinstance(n, int) else eng.to_reg(n) for _, n in events]
            eng.wait_ge(ones_ok, 3)
            for (s, _), n in zip(events, values):
                need(eng, s, n)

        def need(eng, s, n):
            if not isinstance(n, int) or n > 0:
                eng.wait_ge(s, n)

        def reader(stage, a):
            return {
                "x1_t": lambda: (x1t_sb, 4, 2 * a[0] + a[1]),
                "qk": lambda: (qk_x, 8, a[0]),
                "v": lambda: (v_sb, 4, a[0]),
                "max_rows": lambda: (mt_sb, 4, a[0]),
                "out_norm": lambda: (ctx_ok, 8, 2 * a[0] + a[1]),
                "ctx_t": lambda: (ct_sb, 4, 2 * a[0] + a[1]),
                "out_proj": lambda: (h_ok, 4, 2 * a[0] + a[1]),
                "x2_t": lambda: (x2t_sb, 4, 2 * a[0] + a[1]),
                "fc1_u": lambda: (u_sb, 2, a[0]),
                "fc1_v": lambda: (hid_raw, 16, F * a[0] + a[1]),
                "fc2_u": lambda: (w_sb, 2, a[0]),
                "fc2_v": lambda: (y_ok, 4, 2 * a[0] + a[1]),
                "zq_t": lambda: (zt_sb, 4, 2 * a[0] + a[1]),
                "ffn": lambda: (ffn_y, 4, 2 * a[0] + a[1]),
            }.get(stage, lambda: None)()

        uses = [n for n, (_, stage, a) in enumerate(SCHED) if reader(stage, a)]
        assert len(uses) % 2 == 0 and all(SCHED[n][0] >= 0 for n in uses[-2:])
        bank_of = {n: k % 2 for k, n in enumerate(uses)}

        def runs(s, n):
            return not isinstance(s, int) or 0 <= s + SCHED[n][0] < B

        def x_read(s, n):
            same = [m for m in uses if bank_of[m] == bank_of[n]]
            for back, places in ((0, [m for m in same if m < n]), (1, same), (2, same)):
                before = s - back
                valid = [m for m in places if runs(before, m)]
                if valid:
                    db, stage, a = SCHED[valid[-1]]
                    who, per, k = reader(stage, a)
                    return who, (before + db) * per + k + 1
            return None

        def run_steps(eng, stages):
            def step(s):
                for n, (db, stage, a) in enumerate(SCHED):
                    if stage in stages and runs(s, n):
                        if n in bank_of:
                            stages[stage]((s, n), s + db, *a)
                        else:
                            stages[stage](s + db, *a)
            step(-1)
            step(0)
            step(1)
            with eng.Fori(2, B - 1) as s:
                step(s)
            step(B - 1)
            step(B)

        def st_width(st):
            c, j = STEPS[st]
            return c, j, max(0, P * (j - TH * c))

        block = ctx.enter_context(nc.Block())

        @block.sync
        def _(sp):
            for name, k, u, v in (("q_in", 0, q_U, q_V), ("k_in", 1, k_U, k_V), ("v_in", 2, v_U, v_V)):
                sp.dma_start(u_raw[k], u.rearrange("(c p) h r -> p c (h r)", p=P)).then_inc(loaded[name], 16)
                sp.dma_start(v_raw[k].rearrange("r (h e) -> r h e", h=H), v.rearrange("h r e -> r h e")).then_inc(loaded[name], 16)
            sp.dma_start(ou_raw, out_U.rearrange("(c p) r -> p c r", p=P)).then_inc(loaded["out_in"], 16)
            sp.dma_start(ov_raw[0], out_V[0:P, :]).then_inc(loaded["out_in"], 16)
            sp.dma_start(ov_raw[1], out_V[P:R_OUT, :]).then_inc(loaded["out_in"], 16)
            for dst, src in (
                (g1, ln1_g.rearrange("(c p) -> p c", p=P)), (b1, ln1_b.rearrange("(c p) -> p c", p=P)),
                (g2, ln2_g.rearrange("(c p) -> p c", p=P)), (bb2, ln2_b.rearrange("(c p) -> p c", p=P)),
                (qb, q_b.rearrange("(f h) e -> (h e) f", f=2)), (kb, k_b.rearrange("(f h) e -> (h e) f", f=2)),
                (fc1b, fc1_b.rearrange("(f p) -> p f", p=P)),
                (vb, v_b.rearrange("h e -> (h e)").partition_broadcast(P)),
                (ob, out_b.partition_broadcast(P)), (b2, fc2_b.partition_broadcast(P)),
                (fb, ffn_bias.partition_broadcast(P)),
                (sc[:, 0:1], in_scale.partition_broadcast(P)), (sc[:, 1:2], w_scale.partition_broadcast(P)),
                (w1u, fc1_U.rearrange("(c p) r -> p c r", p=P)), (w1v, fc1_V),
                (w2u, fc2_U.rearrange("(f p) r -> p f r", p=P)), (w2v, fc2_V),
                (wf_raw, ffn_w.rearrange("(c p) n -> p c n", p=P)),
            ):
                with nc.allow_non_contiguous_dma(reason="a few short vectors, one element per partition"):
                    sp.dma_start(dst if isinstance(dst, bass.AP) else dst[:], src).then_inc(loaded["rest_in"], 16)

            def load_x(b, hf):
                need_first(sp, (x1t_pe, b * 4 + 2 * hf))
                sp.dma_start(x_in[:, :, :], hidden[b, hf * HALF:(hf + 1) * HALF, :].rearrange("(t p) d -> p t d", p=P)).then_inc(x_loaded, 16)

            def load_res(b, hf):
                need_first(sp, (y_ok, b * 4 + 2 * hf))
                sp.dma_start(x_res[:, :, :], hidden[b, hf * HALF:(hf + 1) * HALF, :].rearrange("(t p) d -> p t d", p=P)).then_inc(res_loaded, 16)

            def place(b, g):
                done = b * 8 + 4 * (g // 2) + 4
                need_first(sp, (qk_lo, done), (qk_mid, done), (qk_hi, done),
                           (scores_pe, (b - 1) * G * NST * HG + (g + 1) * NST * HG))
                sp.wait_ge(fold_sb, 7)
                sp.wait_ge(wf_ok, 7)
                both = parts[:, :, :, :].rearrange("p w n s -> p (w n) s")
                for hh in range(HG):
                    lo = (g % 2 * HG + hh) * DH
                    for r in range(SPLIT):
                        qp, kp = Q_PARTS[r], 3 + K_PARTS[r]
                        sp.dma_start(slots[DH * r:DH * (r + 1), g, hh, :, :],
                                     both[lo:lo + DH, qp:kp + 1:kp - qp, :]).then_inc(placed[g], 16)

            def max_rows(xn, b, g):
                need(sp, mt_sb, b * G + g + 1)
                for hh in range(HG):
                    sp.dma_start(qs[KS:KM, g, hh, :], m_rows[MROWS * hh:MROWS * (hh + 1), :]).then_inc(m_placed, 16)

            def store(b, hf):
                need_first(sp, (ln[4]["norm"], b * 8 + 4 * hf + 4))
                sp.dma_start(out[b, hf * HALF:(hf + 1) * HALF, :].rearrange("(t p) d -> p t d", p=P), h_sb[:, :, :]).then_inc(stored, 16)

            run_steps(sp, {"load_x": load_x, "load_res": load_res, "place": place, "max_rows": max_rows, "store": store})
            sp.wait_ge(stored, 2 * B * 16)

        @block.gpsimd
        def _(pool):
            pool.memset(ident[:, :], 0.0).then_inc(ident_ok, 1)
            pool.memset(ident_b[:, :], 0.0).then_inc(ident_ok, 1)
            pool.wait_ge(ident_ok, 2)
            for m in (ident, ident_b):
                pool.affine_select(out=m[:, :], in_=m[:, :], compare_op=ALU.not_equal, fill=1.0, base=0,
                                   pattern=[[-1, P]], channel_multiplier=1).then_inc(ident_ok, 1)
            pool.memset(mask[:, :], 0.0).then_inc(mask_ok, 1)
            pool.wait_ge(mask_ok, 1)
            pool.affine_select(out=mask[:, HALF - P:HALF], in_=mask[:, HALF - P:HALF], compare_op=ALU.is_ge, fill=NEG,
                               base=0, pattern=[[-1, P]], channel_multiplier=1).then_inc(mask_ok, 1)
            pool.memset(mask_t[:, :], 0.0).then_inc(mask_ok, 1)
            pool.wait_ge(mask_ok, 3)
            pool.affine_select(out=mask_t[:, :], in_=mask_t[:, :], compare_op=ALU.is_ge, fill=NEG,
                               base=0, pattern=[[1, P]], channel_multiplier=-1).then_inc(mask_ok, 1)
            pool.memset(half_neg[:, :], -0.5).then_inc(ones_ok, 1)
            pool.memset(vs[:, :, :, DH:DH + 1], 1.0).then_inc(ones_ok, 1)

            def power(n):
                def f(b, hf):
                    need(pool, ln[n]["norm"], b * 8 + 4 * hf)
                    need(pool, ln[n]["var"], b * 2 + hf + 1)
                    pool.tensor_tensor(rstd[n][:, :], var_eps[n][:, :], half_neg[:, :], ALU.pow).then_inc(ln[n]["rstd"], 1)
                return f

            def qk(xn, b, n):
                w, hf = n % 4 // 2, n % 2
                cols = slice(hf * HALF, (hf + 1) * HALF)
                need(pool, qk_x, b * 8 + n + 1)
                need(pool, qk_lo, b * 8 + n)
                need(pool, qk_hi, b * 8 + n + 1)
                pool.tensor_tensor(qk_rest[:, :], qk_full[:, :], parts[:, w, 0, cols], ALU.subtract).then_inc(qk_r, 1)
                need(pool, qk_mid, b * 8 + n + 1)
                pool.tensor_tensor(parts[:, w, 2, cols], qk_rest[:, :], parts[:, w, 1, cols], ALU.subtract).then_inc(qk_lo, 1)

            def load_res(b, hf):
                need(pool, res_loaded, (b * 2 + hf + 1) * 16)
                need(pool, stored, (b * 2 + hf) * 16)
                need(pool, loaded["rest_in"], 18 * 16)
                for t in range(TH):
                    pool.tensor_tensor(h_sb[:, t, :], x_res[:, t, :], ob[:, :], ALU.add).then_inc(res_ob, 1)
                need(pool, res_ob, (b * 2 + hf + 1) * TH)
                for t in range(TH):
                    pool.tensor_tensor(x_res[:, t, :], x_res[:, t, :], b2[:, :], ALU.add).then_inc(res_b2, 1)

            def fc1_u(xn, b, hf):
                need(pool, h_ok, b * 4 + 2 * hf + 2)
                need(pool, res_b2, (b * 2 + hf + 1) * TH)
                xr, hx = x_res[:, :, :].rearrange(flat), h_sb[:, :, :].rearrange(flat)
                pool.tensor_tensor(xr, xr, hx, ALU.add).then_inc(res_h, 1)

            def quant(b, hf):
                k = b * 2 + hf
                need(pool, quant_v, k * 5 + 4)
                pool.tensor_tensor(q_t, q_v, q_m, ALU.add).then_inc(quant_p, 1)
                need(pool, quant_p, k * 3 + 1)
                pool.tensor_tensor(q_t, q_t, q_m, ALU.subtract).then_inc(quant_p, 1)
                need(pool, quant_v, k * 5 + 5)
                need(pool, zt_pe, k * C)
                pool.tensor_tensor(zq[:, :, :].rearrange(flat), q_t, q_n, ALU.add).then_inc(quant_p, 1)

            def ffn(xn, b, hf, pr):
                k = b * 4 + 2 * hf + pr
                need(pool, ffn_y, k + 1)
                pair = slice(2 * pr, 2 * pr + 2)
                for t in (2 * pr, 2 * pr + 1):
                    pool.tensor_tensor(yb[:, t, :], yb[:, t, :], fb[:, :], ALU.add).then_inc(ffn_b, 1)
                need(pool, ffn_b, k * 2 + 2)
                pool.tensor_tensor(h_sb[:, pair, :].rearrange(flat), x2[:, pair, :].rearrange(flat),
                                   yb[:, pair, :].rearrange(flat), ALU.add).then_inc(ffn_sum, 1)

            run_steps(pool, {"ln1_stats": power(1), "ln2_stats": power(2), "ln3_stats": power(3), "ln4_stats": power(4),
                             "qk": qk, "load_res": load_res, "fc1_u": fc1_u, "quant": quant, "ffn": ffn})

        @block.scalar
        def _(act):
            act.wait_ge(loaded["rest_in"], 18 * 16)

            def x1_t(xn, b, hf, ch):
                need(act, x1t_pe, b * 4 + 2 * hf + ch + 1)
                need(act, v_pe, b * 4)
                need(act, qk_pe, b * 8)
                act.activation(x1t[:, ch, hf * HALF:(hf + 1) * HALF], px[bank_of[xn[1]]][:, :], ACT.Identity,
                               bias=b1[:, ch:ch + 1], scale=g1[:, ch:ch + 1]).then_inc(x1t_sb, 1)

            def qk(xn, b, n):
                f, w, hf = n // 4, n % 4 // 2, n % 2
                cols = slice(hf * HALF, (hf + 1) * HALF)
                bias = (qb, kb)[w][:, f:f + 1]
                need(act, qk_pe, b * 8 + n + 1)
                for g in range(G):
                    if g // 2 != f:
                        need(act, placed[g], (b if f else b) * 16 * HG * SPLIT if not f else (b + 1) * 16 * HG * SPLIT)
                act.activation(parts[:, w, 0, cols], px[bank_of[xn[1]]][:, :], ACT.Identity, bias=bias).then_inc(qk_hi, 1)
                need(act, qk_r, b * 8 + n)
                act.activation(qk_full[:, :], px[bank_of[xn[1]]][:, :], ACT.Identity, bias=bias).then_inc(qk_x, 1)

            def max_rows(xn, b, g):
                need(act, mt_pe, b * 4 + g + 1)
                need(act, m_placed, (b * 4 + g) * HG * 16)
                act.activation(m_rows[:, :], px[bank_of[xn[1]]][0:MROWS * HG, :].bitcast(BF16), ACT.Copy).then_inc(mt_sb, 1)

            def scores(b, g, st, hh):
                c, j, lo = st_width(st)
                step = g * NST + st
                n = step * HG + hh
                need(act, scores_pe, b * G * NST * HG + n + 1)
                need(act, pv_pe, b * G * NST + step - NPT + 1)
                act.activation(probs[:, step % NPT, hh, lo:HALF], ps[n % S_RING][:, lo:HALF], ACT.Exp,
                               scale=SCALE).then_inc(exp_done, 1)

            def out_copy(b, g, c):
                k = 2 * g + c
                need(act, pv_pe, b * G * NST + g * NST + (NST if c else TH))
                need(act, o_t, b * 8 + k)
                act.activation(o_sb[:, :], po[:, :], ACT.Copy).then_inc(o_copied, 1)

            def ctx_tr(xn, b, hf, ch):
                need(act, ct_pe, b * 4 + 2 * hf + ch + 1)
                need(act, op_pe, b * 4)
                act.activation(ctx_t[:, hf, ch, :], px[bank_of[xn[1]]][:, :], ACT.Copy).then_inc(ct_sb, 1)

            def x2_t(xn, b, hf, ch):
                need(act, x2t_pe, b * 4 + 2 * hf + ch + 1)
                need(act, u_pe, b * 2 + hf)
                act.activation(x2t[:, ch, :], px[bank_of[xn[1]]][:, :], ACT.Identity,
                               bias=bb2[:, ch:ch + 1], scale=g2[:, ch:ch + 1]).then_inc(x2t_sb, 1)

            def fc1_u(xn, b, hf):
                need(act, u_pe, b * 2 + hf + 1)
                need(act, hid_pe, (b * 2 + hf) * F)
                act.activation(u_t[:, :], px[bank_of[xn[1]]][:, :], ACT.Copy).then_inc(u_sb, 1)

            def gelu(b, hf):
                need(act, hid_raw, (b * 2 + hf + 1) * F)
                act.activation(hid[:, :, :].rearrange(flat), hid[:, :, :].rearrange(flat), ACT.Gelu_apprx_tanh).then_inc(hid_ok, 1)

            def fc2_u(xn, b, hf):
                need(act, w_pe, b * 2 + hf + 1)
                need(act, y_pe, (b * 2 + hf) * 2)
                act.activation(w_t[:, :], px[bank_of[xn[1]]][:, :], ACT.Copy).then_inc(w_sb, 1)

            def zq_t(xn, b, hf, ch):
                need(act, zt_pe, b * 4 + 2 * hf + ch + 1)
                need(act, ffn_pe, (b * 2 + hf) * 2)
                act.activation(zqt[:, ch, :], px[bank_of[xn[1]]][:, 0:HALF // 2].bitcast(BF16), ACT.Copy).then_inc(zt_sb, 1)

            def ffn(xn, b, hf, pr):
                k = b * 4 + 2 * hf + pr
                need(act, ffn_pe, k + 1)
                act.wait_ge(scale_ok, 3)
                act.activation(yb[:, 2 * pr:2 * pr + 2, :].rearrange(flat), px[bank_of[xn[1]]][:, :], ACT.Copy,
                               scale=sc[:, 4:5]).then_inc(ffn_y, 1)

            run_steps(act, {"x1_t": x1_t, "qk": qk, "max_rows": max_rows, "scores": scores, "out_copy": out_copy,
                            "ctx_t": ctx_tr, "x2_t": x2_t, "fc1_u": fc1_u, "gelu": gelu, "fc2_u": fc2_u,
                            "zq_t": zq_t, "ffn": ffn})

        @block.tensor
        def _(pe):
            pe.wait_ge(ident_ok, 4)
            for w, name in enumerate(("q_in", "k_in", "v_in")):
                pe.wait_ge(loaded[name], 32)
                for h2 in range(H // 2):
                    n = w * (H // 2) + h2
                    if n >= 4:
                        pe.wait_ge(ut_sb, n - 3)
                    for hl in range(2):
                        for c in range(C):
                            k = 2 * hl + c
                            last = pe.transpose(bank[n % 4][0:R, k * P:(k + 1) * P],
                                                u_raw[w][:, c, (2 * h2 + hl) * R:(2 * h2 + hl + 1) * R], ident[:, :])
                    last.then_inc(ut_pe, 1)
                pe.wait_ge(ut_sb, (w + 1) * (H // 2))
                if w >= 2:
                    pe.wait_ge(fold_sb, w - 1)
                for c in range(C):
                    for h in range(H):
                        last = pe.matmul(bank[4 + w % 2][:, c * D + h * DH:c * D + (h + 1) * DH], ut[:, h, c, :],
                                         v_raw[w][:, h * DH:(h + 1) * DH], start=True, stop=True)
                last.then_inc(fold_pe, 1)
            pe.wait_ge(loaded["out_in"], 48)
            for c in range(C):
                pe.transpose(bank[6][:, c * P:(c + 1) * P], ou_raw[:, c, 0:P], ident[:, :])
                last = pe.transpose(bank[7][0:R_OUT - P, c * P:(c + 1) * P], ou_raw[:, c, P:R_OUT], ident[:, :])
            last.then_inc(fold_pe, 1)
            pe.wait_ge(fold_sb, 5)
            for c in range(C):
                pe.matmul(bank[5][:, c * D:(c + 1) * D], out_t[0][:, c * P:(c + 1) * P], ov_raw[0], start=True, stop=False)
                last = pe.matmul(bank[5][:, c * D:(c + 1) * D], out_t[1][:, c * P:(c + 1) * P], ov_raw[1], start=False, stop=True)
            last.then_inc(fold_pe, 1)
            pe.wait_ge(fold_sb, 6)
            pe.wait_ge(loaded["rest_in"], 18 * 16)
            pe.wait_ge(ones_ok, 3)
            pe.wait_ge(mask_ok, 4)

            def x_bank(xn):
                free = x_read(*xn)
                if free:
                    need(pe, *free)
                return px[bank_of[xn[1]]]

            def turn(x, src, s, idn):
                for t in range(TH):
                    last = pe.transpose(x[:, t * P:(t + 1) * P], src(t), idn[:, :])
                last.then_inc(s, 1)

            def x1_t(xn, b, hf, ch):
                x = x_bank(xn)
                need(pe, ln[1]["norm"], b * 8 + 4 * hf + 4)
                turn(x, lambda t: x_in[:, t, ch * P:(ch + 1) * P], x1t_pe, ident)

            def qk(xn, b, n):
                x = x_bank(xn)
                f, w, hf = n // 4, n % 4 // 2, n % 2
                need(pe, x1t_sb, b * 4 + 2 * hf + 2)
                for ch in range(C):
                    last = pe.matmul(x[:, :], (wq, wk)[w][:, ch, f * P:(f + 1) * P], x1t[:, ch, hf * HALF:(hf + 1) * HALF],
                                     start=(ch == 0), stop=(ch == C - 1))
                last.then_inc(qk_pe, 1)

            def v(xn, b, g):
                x = x_bank(xn)
                need(pe, x1t_sb, b * 4 + 4)
                gd = HG * DH
                for t in range(T):
                    for ch in range(C):
                        last = pe.matmul(x[:, t * gd:(t + 1) * gd], x1t[:, ch, t * P:(t + 1) * P],
                                         wv[:, ch, g * gd:(g + 1) * gd], start=(ch == 0), stop=(ch == C - 1))
                last.then_inc(v_pe, 1)

            def row_max_(b, g, u):
                hh, i, part = UNITS[u]
                n = g * NU + u
                if u == 0:
                    need(pe, placed[g], (b + 1) * 16 * HG * SPLIT)
                need(pe, row_max, b * G * NU + n - A_RING + 1)
                k1 = min((i + 1) * P, (part + 1) * HALF)
                pe.matmul(pa[n % A_RING][:, 0:k1 - part * HALF], qs[0:KS, g, hh, i * P:(i + 1) * P],
                          ks[0:KS, g, hh, part * HALF:k1], start=True, stop=True).then_inc(max_scores, 1)

            def max_rows(xn, b, g):
                x = x_bank(xn)[0:MROWS * HG, :].bitcast(BF16)
                need(pe, neg_max, (b * 4 + g + 1) * 5)
                for i in range(T):
                    last = pe.transpose(x[:, i * P:(i + 1) * P], m_part[:, i, :, :].rearrange(flat), ident_b[:, :])
                last.then_inc(mt_pe, 1)

            def scores(b, g, st, hh):
                c, j, lo = st_width(st)
                n = (g * NST + st) * HG + hh
                if st == 0 and hh == 0:
                    need(pe, m_placed, (b * 4 + g + 1) * HG * 16)
                need(pe, exp_done, b * G * NST * HG + n - S_RING + 1)
                last = pe.matmul(ps[n % S_RING][:, lo:HALF], ks[0:KM, g, hh, j * P:(j + 1) * P],
                                 qs[0:KM, g, hh, c * HALF + lo:(c + 1) * HALF], start=True, stop=st not in DIAG)
                if st in DIAG:
                    last = pe.matmul(ps[n % S_RING][:, lo:lo + P], ident_b[:, :], mask_t[:, :], start=False, stop=True)
                last.then_inc(scores_pe, 1)

            def values(b, g, st):
                c, j, lo = st_width(st)
                step = g * NST + st
                if st == 0:
                    need(pe, v_sb, b * 4 + g + 1)
                if j == 0:
                    need(pe, o_copied, b * 8 + 2 * g + c)
                need(pe, exp_done, (b * G * NST + step) * HG + HG)
                for hh in range(HG):
                    last = pe.matmul(po[32 * hh:32 * hh + DH + 1, lo:HALF], vs[:, j, g * HG + hh, :],
                                     probs[:, step % NPT, hh, lo:HALF], start=(j == 0), stop=(j == TH * (c + 1) - 1))
                last.then_inc(pv_pe, 1)

            def out_norm(xn, b, g, c):
                x = x_bank(xn)
                need(pe, o_copied, b * 8 + 2 * g + c + 1)
                turn(x, lambda t: o_sb[:, t * P:(t + 1) * P], o_t, ident)

            def ctx_tr(xn, b, hf, ch):
                x = x_bank(xn)
                need(pe, ctx_ok, b * 8 + 2 * (G - 1) + hf + 1)
                turn(x, lambda t: ctx_sb[:, TH * hf + t, ch * P:(ch + 1) * P], ct_pe, ident)

            def out_proj(xn, b, hf, pr):
                x = x_bank(xn)
                need(pe, ct_sb, b * 4 + 2 * hf + 2)
                for tt in range(2):
                    for ch in range(C):
                        t = 2 * pr + tt
                        last = pe.matmul(x[:, tt * D:(tt + 1) * D], ctx_t[:, hf, ch, t * P:(t + 1) * P], wo[:, ch, :],
                                         start=(ch == 0), stop=(ch == C - 1))
                last.then_inc(op_pe, 1)

            def x2_t(xn, b, hf, ch):
                x = x_bank(xn)
                need(pe, ln[2]["norm"], b * 8 + 4 * hf + 4)
                turn(x, lambda t: x2[:, t, ch * P:(ch + 1) * P], x2t_pe, ident)

            def fc1_u(xn, b, hf):
                x = x_bank(xn)
                need(pe, x2t_sb, b * 4 + 2 * hf + 2)
                for ch in range(C):
                    last = pe.matmul(x[:, :], w1u[:, ch, :], x2t[:, ch, :], start=(ch == 0), stop=(ch == C - 1))
                last.then_inc(u_pe, 1)

            def fc1_v(xn, b, hf, f):
                x = x_bank(xn)
                need(pe, u_sb, b * 2 + hf + 1)
                pe.matmul(x[:, :], w1v[:, f * P:(f + 1) * P], u_t[:, :], start=True, stop=True).then_inc(hid_pe, 1)

            def fc2_u(xn, b, hf):
                x = x_bank(xn)
                need(pe, hid_ok, b * 2 + hf + 1)
                for f in range(F):
                    last = pe.matmul(x[:, :], w2u[:, f, :], hid[:, f, :], start=(f == 0), stop=(f == F - 1))
                last.then_inc(w_pe, 1)

            def fc2_v(xn, b, hf, pr):
                x = x_bank(xn)
                need(pe, w_sb, b * 2 + hf + 1)
                for tt in range(2):
                    t = 2 * pr + tt
                    last = pe.matmul(x[:, tt * D:(tt + 1) * D], w_t[:, t * P:(t + 1) * P], w2v[:, :], start=True, stop=True)
                last.then_inc(y_pe, 1)

            def zq_t(xn, b, hf, ch):
                x = x_bank(xn)[:, 0:HALF // 2].bitcast(BF16)
                need(pe, quant_p, (b * 2 + hf + 1) * 3)
                turn(x, lambda t: zq[:, t, ch * P:(ch + 1) * P], zt_pe, ident_b)

            def ffn(xn, b, hf, pr):
                x = x_bank(xn)
                pe.wait_ge(wf_ok, 7)
                need(pe, zt_sb, b * 4 + 2 * hf + 2)
                for tt in range(2):
                    t = 2 * pr + tt
                    for ch in range(C):
                        last = pe.matmul(x[:, tt * D:(tt + 1) * D], zqt[:, ch, t * P:(t + 1) * P], wf[:, ch, :],
                                         start=(ch == 0), stop=(ch == C - 1))
                last.then_inc(ffn_pe, 1)

            run_steps(pe, {"x1_t": x1_t, "qk": qk, "v": v, "row_max": row_max_, "max_rows": max_rows, "scores": scores,
                           "values": values, "out_norm": out_norm, "ctx_t": ctx_tr, "out_proj": out_proj, "x2_t": x2_t,
                           "fc1_u": fc1_u, "fc1_v": fc1_v, "fc2_u": fc2_u, "fc2_v": fc2_v, "zq_t": zq_t, "ffn": ffn})

        @block.vector
        def _(dve):
            dve.memset(po[:, :], 0.0).then_inc(fold_sb, 1)
            for w in range(3):
                for h2 in range(H // 2):
                    n = w * (H // 2) + h2
                    dve.wait_ge(ut_pe, n + 1)
                    if h2 == 0 and w:
                        dve.wait_ge(fold_pe, w)
                    dve.tensor_copy(ut[:, 2 * h2:2 * h2 + 2, :, :].rearrange("p h c d -> p (h c d)"),
                                    bank[n % 4][0:R, :]).then_inc(ut_sb, 1)
                dve.wait_ge(fold_pe, w + 1)
                dve.tensor_copy((wq, wk, wv)[w][:, :, :].rearrange(flat), bank[4 + w % 2][:, :]).then_inc(fold_sb, 1)
            dve.wait_ge(fold_pe, 4)
            dve.tensor_copy(out_t[0], bank[6][:, 0:D])
            dve.tensor_copy(out_t[1], bank[7][0:R_OUT - P, 0:D]).then_inc(fold_sb, 1)
            dve.wait_ge(fold_pe, 5)
            dve.tensor_copy(wo[:, :, :].rearrange(flat), bank[5][:, :]).then_inc(fold_sb, 1)
            dve.wait_ge(fold_sb, 6)
            dve.memset(po[:, :], 0.0).then_inc(fold_sb, 1)
            dve.wait_ge(loaded["rest_in"], 18 * 16)
            dve.reciprocal(sc[:, 2:3], sc[:, 0:1]).then_inc(scale_ok, 1)
            dve.reciprocal(sc[:, 3:4], sc[:, 1:2]).then_inc(scale_ok, 1)
            dve.tensor_tensor(sc[:, 4:5], sc[:, 0:1], sc[:, 1:2], ALU.mult).then_inc(scale_ok, 1)
            dve.wait_ge(scale_ok, 3)
            wv_, wm, wt, wn = (a[:, 0:C * D] for a in (q_v, q_m, q_t, q_n))
            dve.tensor_scalar(wv_, wf_raw[:, :, :].rearrange(flat), sc[:, 3:4], None, ALU.mult).then_inc(wf_ok, 1)
            dve.wait_ge(wf_ok, 1)
            dve.tensor_scalar(wm.bitcast(U32), wv_.bitcast(U32), 0x7F800000, None, ALU.bitwise_and).then_inc(wf_ok, 1)
            dve.wait_ge(wf_ok, 2)
            dve.tensor_scalar(wm, wm, 2.0 ** -6, 1.5 * 2.0 ** 20, ALU.max, ALU.mult).then_inc(wf_ok, 1)
            dve.wait_ge(wf_ok, 3)
            dve.tensor_tensor(wt, wv_, wm, ALU.add).then_inc(wf_ok, 1)
            dve.wait_ge(wf_ok, 4)
            dve.tensor_tensor(wt, wt, wm, ALU.subtract).then_inc(wf_ok, 1)
            dve.wait_ge(wf_ok, 5)
            dve.tensor_scalar(wn, wt, 7.4e35, 0.0, ALU.mult, ALU.mult).then_inc(wf_ok, 1)
            dve.wait_ge(wf_ok, 6)
            dve.tensor_tensor(wf[:, :, :].rearrange(flat), wt, wn, ALU.add).then_inc(wf_ok, 1)
            dve.wait_ge(wf_ok, 7)
            dve.memset(ks[KS:KM, :, :, :].bitcast(F32), float(np.uint32(0x3F803F80).view(np.float32))).then_inc(ones_ok, 1)

            def stats(n, buf, ready):
                def f(b, hf):
                    s = ln[n]
                    k = b * 2 + hf
                    need(dve, *ready(b, hf))
                    need(dve, s["aggr"], k * TH)
                    for t in range(TH):
                        dve.bn_stats(st6[n][:, t, :], buf[:, t, :]).then_inc(s["stats"], 1)
                    need_first(dve, (s["stats"], (k + 1) * TH), (s["norm"], k * TH), (s["var"], k))
                    for t in range(TH):
                        dve.bn_aggr(mv[n][:, t, :], st6[n][:, t, :]).then_inc(s["aggr"], 1)
                    need(dve, s["aggr"], (k + 1) * TH)
                    need(dve, s["rstd"], k)
                    dve.tensor_scalar(var_eps[n][:, :], mv[n][:, :, 1], EPS, None, ALU.add).then_inc(s["var"], 1)
                return f

            def apply(n, src, dst, free):
                def f(b, hf):
                    s = ln[n]
                    k = b * 2 + hf
                    need(dve, s["rstd"], k + 1)
                    if free:
                        need(dve, *free(b, hf))
                    for t in range(TH):
                        dve.tensor_scalar(dst[:, t, :], src[:, t, :], mv[n][:, t, 0:1], rstd[n][:, t:t + 1],
                                          ALU.subtract, ALU.mult).then_inc(s["norm"], 1)
                return f

            def qk(xn, b, n):
                w, hf = n % 4 // 2, n % 2
                need(dve, qk_r, b * 8 + n + 1)
                dve.tensor_copy(parts[:, w, 1, hf * HALF:(hf + 1) * HALF], qk_rest[:, :]).then_inc(qk_mid, 1)

            def v(xn, b, g):
                need(dve, v_pe, b * 4 + g + 1)
                need(dve, pv_pe, (b - 1) * G * NST + (g + 1) * NST)
                gd = HG * DH
                x = px[bank_of[xn[1]]]
                for t in range(T):
                    last = dve.tensor_tensor(vs[:, t, g * HG:(g + 1) * HG, 0:DH],
                                             x[:, t * gd:(t + 1) * gd].rearrange("p (h e) -> p h e", h=HG),
                                             vb[:, g * gd:(g + 1) * gd].rearrange("p (h e) -> p h e", h=HG), ALU.add)
                last.then_inc(v_sb, 1)

            def row_max_(b, g, u):
                hh, i, part = UNITS[u]
                n = g * NU + u
                k = b * G * NU + n
                if u == 0:
                    need(dve, neg_max, (b * 4 + g) * 5)
                need(dve, row_max, k - TRASH + 1)
                need_first(dve, (max_scores, k + 1))
                dst = (mx_hi[:, i - TH, hh:hh + 1] if part else mx[:, i, hh:hh + 1])
                if i >= TH and part == 0:
                    dve.tensor_reduce(dst, pa[n % A_RING][:, :], AX.X, ALU.max).then_inc(row_max, 1)
                else:
                    w = (i + 1) * P - part * HALF
                    dve.tensor_tensor_reduce(trash[:, n % TRASH, 0:w], pa[n % A_RING][:, 0:w], mask[:, HALF - w:HALF],
                                             1.0, 3.0 * NEG, ALU.add, ALU.max, dst).then_inc(row_max, 1)

            def max_parts(b, g):
                k = (b * 4 + g) * 5
                need(dve, row_max, (b * G + g + 1) * NU)
                dve.tensor_tensor(mx[:, TH:T, :], mx[:, TH:T, :], mx_hi[:, :, :], ALU.max).then_inc(neg_max, 1)
                need(dve, neg_max, k + 1)
                need(dve, mt_pe, b * 4 + g)
                dve.tensor_scalar(m_part[:, :, :, 0], mx[:, :, :], -1.0, None, ALU.mult).then_inc(neg_max, 1)
                need(dve, neg_max, k + 2)
                dve.scalar_tensor_tensor(out=m_rest[:, :, :], in0=mx[:, :, :], scalar=-1.0, in1=m_part[:, :, :, 0],
                                         op0=ALU.mult, op1=ALU.subtract).then_inc(neg_max, 1)
                need(dve, neg_max, k + 3)
                dve.tensor_copy(m_part[:, :, :, 1], m_rest[:, :, :]).then_inc(neg_max, 1)
                need(dve, neg_max, k + 4)
                dve.tensor_tensor(m_part[:, :, :, 2], m_rest[:, :, :], m_part[:, :, :, 1], ALU.subtract).then_inc(neg_max, 1)

            def out_norm(xn, b, g, c):
                k = b * 8 + 2 * g + c
                x = px[bank_of[xn[1]]][:, :].rearrange("p (t h e) -> p t h e", t=TH, h=HG)
                need(dve, o_t, k + 1)
                need(dve, ctx_ok, k)
                dve.reciprocal(rden[:, :, :, :], x[:, :, :, DH:DH + 1]).then_inc(o_rden, 1)
                need(dve, o_rden, k + 1)
                need(dve, ct_pe, (b - 1) * 4 + 2 * c + 2)
                dst = ctx_sb[:, TH * c:TH * (c + 1), g * HG * DH:(g + 1) * HG * DH].rearrange("p t (h e) -> p t h e", h=HG)
                dve.tensor_tensor(dst, x[:, :, :, 0:DH], rden[:, :, :, :].to_broadcast([P, TH, HG, DH]),
                                  ALU.mult).then_inc(ctx_ok, 1)

            def out_proj(xn, b, hf, pr):
                k = b * 4 + 2 * hf + pr
                need(dve, op_pe, k + 1)
                need(dve, res_ob, (b * 2 + hf + 1) * TH)
                dst = h_sb[:, 2 * pr:2 * pr + 2, :].rearrange(flat)
                dve.tensor_tensor(dst, px[bank_of[xn[1]]][:, :], dst, ALU.add).then_inc(h_ok, 1)

            def fc1_v(xn, b, hf, f):
                k = b * 2 + hf
                need(dve, hid_pe, k * F + f + 1)
                need(dve, w_pe, k)
                need(dve, quant_p, k * 3)
                dve.tensor_scalar(hid[:, f, :], px[bank_of[xn[1]]][:, :], fc1b[:, f:f + 1], None, ALU.add).then_inc(hid_raw, 1)

            def fc2_v(xn, b, hf, pr):
                need(dve, y_pe, b * 4 + 2 * hf + pr + 1)
                need(dve, res_h, b * 2 + hf + 1)
                pair = slice(2 * pr, 2 * pr + 2)
                dve.tensor_tensor(h_sb[:, pair, :].rearrange(flat), px[bank_of[xn[1]]][:, :],
                                  x_res[:, pair, :].rearrange(flat), ALU.add).then_inc(y_ok, 1)

            def quant(b, hf):
                k = (b * 2 + hf) * 5
                dve.wait_ge(scale_ok, 3)
                need(dve, ln[3]["norm"], (b * 2 + hf + 1) * TH)
                need(dve, w_pe, b * 2 + hf + 1)
                need(dve, ffn_sum, (b * 2 + hf) * 2)
                z16 = yb[:, :, :].rearrange(flat)
                dve.tensor_copy(z16, x2[:, :, :].rearrange(flat)).then_inc(quant_v, 1)
                need(dve, quant_v, k + 1)
                dve.tensor_scalar(q_v, z16, sc[:, 2:3], None, ALU.mult).then_inc(quant_v, 1)
                need(dve, quant_v, k + 2)
                dve.tensor_scalar(q_m.bitcast(U32), q_v.bitcast(U32), 0x7F800000, None, ALU.bitwise_and).then_inc(quant_v, 1)
                need(dve, quant_v, k + 3)
                dve.tensor_scalar(q_m, q_m, 2.0 ** -6, 1.5 * 2.0 ** 20, ALU.max, ALU.mult).then_inc(quant_v, 1)
                need(dve, quant_p, (b * 2 + hf) * 3 + 2)
                dve.tensor_scalar(q_n, q_t, 7.4e35, 0.0, ALU.mult, ALU.mult).then_inc(quant_v, 1)

            run_steps(dve, {
                "ln1_stats": stats(1, x_in, lambda b, hf: (x_loaded, (b * 2 + hf + 1) * 16)),
                "ln1_apply": apply(1, x_in, x_in, None),
                "ln2_stats": stats(2, h_sb, lambda b, hf: (h_ok, b * 4 + 2 * hf + 2)),
                "ln2_apply": apply(2, h_sb, x2, lambda b, hf: (ffn_sum, (b * 2 + hf) * 2)),
                "ln3_stats": stats(3, h_sb, lambda b, hf: (y_ok, b * 4 + 2 * hf + 2)),
                "ln3_apply": apply(3, h_sb, x2, lambda b, hf: (x2t_pe, b * 4 + 2 * hf + 2)),
                "ln4_stats": stats(4, h_sb, lambda b, hf: (ffn_sum, b * 4 + 2 * hf + 2)),
                "ln4_apply": apply(4, h_sb, h_sb, None),
                "qk": qk, "v": v, "row_max": row_max_, "max_parts": max_parts, "out_norm": out_norm,
                "out_proj": out_proj, "fc1_v": fc1_v, "fc2_v": fc2_v, "quant": quant})


_INS = ["L0_attn_hidden_states", "L0_attn_ln1_g", "L0_attn_ln1_b", "L0_attn_ln2_g", "L0_attn_ln2_b",
        "L0_attn_q_U", "L0_attn_q_V", "L0_attn_q_b", "L0_attn_k_U", "L0_attn_k_V", "L0_attn_k_b",
        "L0_attn_v_U", "L0_attn_v_V", "L0_attn_v_b", "L0_attn_out_U", "L0_attn_out_V", "L0_attn_out_b",
        "L0_attn_fc1_U", "L0_attn_fc1_V", "L0_attn_fc1_b", "L0_attn_fc2_U", "L0_attn_fc2_V", "L0_attn_fc2_b",
        "L0_ffn_kernel", "L0_ffn_input_scale", "L0_ffn_kernel_scale", "L0_ffn_bias"]


def kernel(**inputs):
    import numpy as _np
    import concourse.bacc as _bacc
    from concourse import mybir as _mybir
    from concourse.bass_utils import run_bass_kernel_spmd as _run

    nc = _bacc.Bacc("TRN2", target_bir_lowering=False, num_devices=1)
    arrays, args = {}, []
    for name in _INS:
        a = _np.ascontiguousarray(inputs[name])
        arrays[f"in_{name}"] = a
        args.append(nc.dram_tensor(f"in_{name}", a.shape, _mybir.dt.from_np(a.dtype), kind="ExternalInput").ap())
    args.append(nc.dram_tensor("out_0", (B, S, D), _mybir.dt.float32, kind="ExternalOutput").ap())
    build(nc, *args)
    r = _run(nc, [arrays], core_ids=[0])
    return r.results[0]["out_0"]
```

```python
from contextlib import ExitStack

import numpy as np

import concourse.bass as bass
from concourse import mybir

ALU = mybir.AluOpType
ACT = mybir.ActivationFunctionType
AX = mybir.AxisListType
F32 = mybir.dt.float32
BF16 = mybir.dt.bfloat16
U32 = mybir.dt.uint32

P = 128
B, S, D = 8, 1024, 256
H, DH, R = 16, 16, 48
R_OUT, R_MLP, FF = 192, 128, 1024
T = S // P
C = D // P
HALF = S // 2
TH = T // 2
F = FF // P
G = 4
HG = H // G
SPLIT = 6
KS = SPLIT * DH
MROWS = 3
KM = KS + MROWS
Q_PARTS = (0, 0, 0, 1, 1, 2)
K_PARTS = (0, 1, 2, 0, 1, 0)
EPS = 1e-5
NEG = -1.0e30
SCALE = DH ** -0.5

STEPS = [(c, j) for c in range(2) for j in range(TH * (c + 1))]
NST = len(STEPS)
UNITS = [(hh, i, part) for hh in range(HG) for i in range(T) for part in range(1 + (i >= TH))]
NU = len(UNITS)
PER_STEP = NU // NST
A_RING, S_RING, NPT, TRASH = 3, 2, 2, 2
DIAG = [n for n, (c, j) in enumerate(STEPS) if j >= TH * c]


def schedule():
    slots = G * NST * HG
    more = [[] for _ in range(slots)]
    bank_use = [None] * slots

    def put(n, db, stage, *args):
        more[n].append((db, stage, args))
        return n

    def put_x(n, db, stage, *args, parts=1, out=True):
        while any(bank_use[n:n + parts]):
            n += 1
        for k in range(parts):
            bank_use[n + k] = (db, stage, args + ((k,) if parts > 1 else ()))
        if out:
            put(n + parts, db, stage + ".out", *args)
        return n + parts

    def norm(n, db, which, hf):
        for t in range(0, TH, 2):
            put(n + t // 2, db, f"ln{which}_stats", hf, t)
        put(n + 2, db, f"ln{which}_aggr", hf)
        for t in range(0, TH, 2):
            put(n + 5 + t // 2, db, f"ln{which}_apply", hf, t)
        return n + 6

    def split(n, db, k):
        n = put_x(n, db, "qk", k)
        put(n + 2, db, "qk_parts", k)
        return n + 2

    block = NST * HG
    for g in range(G):
        for c in range(2):
            done = g * block + HG * (TH if c == 0 else NST) + 2
            if done < slots:
                put_x(done, 0, "out_norm", g, c)
            else:
                put_x(done - slots, -1, "out_norm", g, c)
    for n, db, g in ((0, 0, 1), (block, 0, 2), (2 * block, 0, 3), (3 * block, 1, 0)):
        put_x(n + 3, db, "max_rows", g)
    put(0, 1, "load_x", 0)
    put(0, -1, "load_res", 0)
    put(0, 0, "place", 3)
    n = norm(4, 1, 1, 0)
    put_x(5, 0, "v", 3, parts=2)
    for ch in range(C):
        n = put_x(n, 1, "x1_t", 0, ch)
    put(n, 1, "load_x", 1)
    n = norm(n + 5, 1, 1, 1)
    for ch in range(C):
        n = put_x(n, 1, "x1_t", 1, ch)
    n += 1
    for k in range(4):
        n = split(n, 1, k)
    assert n <= block
    put(block, 1, "place", 0)
    put(2 * block, 1, "place", 1)
    n = 2 * block + 12
    for k in range(4, 8):
        n = split(n, 1, k)
    assert n <= 3 * block
    put(3 * block, 1, "place", 2)
    for g, n in ((0, block + 10), (1, slots - 7), (2, slots - 4)):
        put_x(n, 1, "v", g, parts=2)
    for hf, n in ((0, 4), (1, 6)):
        for ch in range(C):
            n = put_x(n, -1, "ctx_t", hf, ch)
    n = 8
    for hf in range(2):
        if hf:
            put(n, -1, "load_res", hf)
        put(n if hf == 0 else n + 5, -1, "add_biases", hf)
        n = n + 3 if hf == 0 else n + 9
        for pr in range(2):
            n = put_x(n, -1, "out_proj", hf, pr)
        n = norm(n + 1, -1, 2, hf)
        for ch in range(C):
            n = put_x(n, -1, "x2_t", hf, ch)
        n = put_x(n + 1, -1, "fc1_u", hf)
        n += 1
        for f in range(F):
            n = put_x(n, -1, "fc1_v", hf, f)
        put(n + 1, -1, "gelu", hf)
        n = put_x(n + 6, -1, "fc2_u", hf, parts=4)
        n += 1
        for pr in range(2):
            n = put_x(n, -1, "fc2_v", hf, pr)
        n = norm(n + 1, -1, 3, hf)
        put(n, -1, "quant", hf, 0)
        put(n + 1, -1, "quant", hf, 1)
        put(n + 6, -1, "quant", hf, 2)
        n += 9
        for ch in range(C):
            n = put_x(n, -1, "zq_t", hf, ch)
        n += 1
        for pr in range(2):
            n = put_x(n, -1, "ffn", hf, pr)
        n = norm(n + 4, -1, 4, hf)
        put(n, -1, "store", hf)

    out = []
    for n in range(slots):
        step, hh = divmod(n, HG)
        g, st = divmod(step, NST)
        out.append((0, "scores", (g, st, hh)))
        db, ga = (0, g + 2) if g < 2 else (1, g - 2)
        out.append((db, "row_max", (ga, st * HG + hh)))
        if n % block == block - 1:
            out.append((db, "max_parts", (ga,)))
        if hh == 1:
            db, m = (0, step - 1) if step else (-1, G * NST - 1)
            out.append((db, "values", divmod(m, NST)))
            c, j = STEPS[m % NST]
            if j == TH * (c + 1) - 1:
                out.append((db, "out_copy", (m // NST, c)))
        out += more[n]
        if bank_use[n]:
            out.append(bank_use[n])
    return out


def build(nc, hidden, ln1_g, ln1_b, ln2_g, ln2_b, q_U, q_V, q_b, k_U, k_V, k_b, v_U, v_V, v_b,
          out_U, out_V, out_b, fc1_U, fc1_V, fc1_b, fc2_U, fc2_V, fc2_b, ffn_w, in_scale, w_scale,
          ffn_bias, out):
    SCHED = schedule()
    with ExitStack() as ctx:
        def sb(name, shape, dt=F32):
            return ctx.enter_context(nc.sbuf_tensor(name, shape, dt))

        def sem(name):
            return ctx.enter_context(nc.semaphore(name))

        slots = sb("slots", [P, G, HG, 2, S], BF16)
        qs, ks = slots[:, :, :, 0, :], slots[:, :, :, 1, :]
        vs = sb("vs", [P, T, H, DH + 1])
        probs = sb("probs", [P, NPT, HG, HALF])
        parts = sb("parts", [P, 2, 3, S], BF16)
        qk_full = sb("qk_full", [P, HALF])
        qk_rest = sb("qk_rest", [P, HALF])
        x_in = sb("x_in", [P, TH, D])
        x1t = sb("x1t", [P, C, S])
        ctx_sb = sb("ctx_sb", [P, T, D])
        ctx_t = sb("ctx_t", [P, 2, C, HALF])
        o_sb = sb("o_sb", [P, HALF])
        x_res = sb("x_res", [P, TH, D])
        h_sb = sb("h_sb", [P, TH, D])
        x2 = sb("x2", [P, TH, D])
        x2t = sb("x2t", [P, C, HALF])
        u_t = sb("u_t", [P, HALF])
        hid = sb("hid", [P, F, HALF])
        w_t = sb("w_t", [P, HALF])
        zq = sb("zq", [P, TH, D], BF16)
        zqt = sb("zqt", [P, C, HALF], BF16)
        yb = sb("yb", [P, TH, D], BF16)
        trash = sb("trash", [P, TRASH, HALF], BF16)
        m_rows = sb("m_rows", [MROWS * HG, S], BF16)
        mx = sb("mx", [P, T, HG])
        mx_hi = sb("mx_hi", [P, TH, HG])
        m_part = sb("m_part", [P, T, HG, MROWS], BF16)
        m_rest = sb("m_rest", [P, T, HG])
        rden = sb("rden", [P, TH, HG, 1])
        LN = range(1, 5)
        st6 = {n: sb(f"st6_{n}", [P, TH, 6]) for n in LN}
        mv = {n: sb(f"mv_{n}", [P, TH, 2]) for n in LN}
        var_eps = {n: sb(f"var_eps_{n}", [P, TH]) for n in LN}
        rstd = {n: sb(f"rstd_{n}", [P, TH]) for n in LN}
        wq = sb("wq", [P, C, D])
        wk = sb("wk", [P, C, D])
        wv = sb("wv", [P, C, D])
        wo = sb("wo", [P, C, D])
        w1u = sb("w1u", [P, C, R_MLP])
        w1v = sb("w1v", [P, FF])
        w2u = sb("w2u", [P, F, R_MLP])
        w2v = sb("w2v", [P, D])
        wf = sb("wf", [P, C, D], BF16)
        vb = sb("vb", [P, D])
        ob = sb("ob", [P, D])
        b2 = sb("b2", [P, D])
        fb = sb("fb", [P, D], BF16)
        g1 = sb("g1", [P, C])
        b1 = sb("b1", [P, C])
        g2 = sb("g2", [P, C])
        bb2 = sb("bb2", [P, C])
        qb = sb("qb", [P, 2])
        kb = sb("kb", [P, 2])
        fc1b = sb("fc1b", [P, F])
        sc = sb("sc", [P, 5])
        ident = sb("ident", [P, P])
        ident_b = sb("ident_b", [P, P], BF16)
        mask = sb("mask", [P, HALF])
        mask_t = sb("mask_t", [P, P], BF16)
        half_neg = sb("half_neg", [P, TH])

        bank = [ctx.enter_context(nc.psum_tensor(f"bank{n}", [P, HALF], F32)) for n in range(8)]
        pa, ps, po, px = bank[0:A_RING], bank[A_RING:5], bank[5], bank[6:8]

        names_in = ["q_in", "k_in", "v_in", "out_in", "rest_in"]
        loaded = {n: sem(n) for n in names_in}
        ident_ok, mask_ok, ones_ok = sem("ident_ok"), sem("mask_ok"), sem("ones_ok")
        ut_pe, ut_sb, fold_pe, fold_sb = sem("ut_pe"), sem("ut_sb"), sem("fold_pe"), sem("fold_sb")
        scale_ok, wf_ok = sem("scale_ok"), sem("wf_ok")
        x_loaded = sem("x_loaded")
        ln = {n: {k: sem(f"ln{n}_{k}") for k in ("stats", "aggr", "var", "rstd", "norm")} for n in LN}
        x1t_pe, x1t_sb = sem("x1t_pe"), sem("x1t_sb")
        qk_pe, qk_hi, qk_x, qk_r, qk_mid, qk_lo = (sem(n) for n in ("qk_pe", "qk_hi", "qk_x", "qk_r", "qk_mid", "qk_lo"))
        placed = [sem(f"placed{g}") for g in range(G)]
        v_pe, v_sb = sem("v_pe"), sem("v_sb")
        max_scores, row_max, neg_max = sem("max_scores"), sem("row_max"), sem("neg_max")
        mt_pe, mt_sb, m_placed = sem("mt_pe"), sem("mt_sb"), sem("m_placed")
        scores_pe, exp_done, pv_pe = sem("scores_pe"), sem("exp_done"), sem("pv_pe")
        o_copied, o_t, o_rden, ctx_ok = sem("o_copied"), sem("o_t"), sem("o_rden"), sem("ctx_ok")
        res_loaded, res_ob, res_b2, res_h = sem("res_loaded"), sem("res_ob"), sem("res_b2"), sem("res_h")
        ct_pe, ct_sb, op_pe, h_ok = sem("ct_pe"), sem("ct_sb"), sem("op_pe"), sem("h_ok")
        x2t_pe, x2t_sb, u_pe, u_sb = sem("x2t_pe"), sem("x2t_sb"), sem("u_pe"), sem("u_sb")
        hid_pe, hid_raw, hid_ok = sem("hid_pe"), sem("hid_raw"), sem("hid_ok")
        w_pe, w_sb, y_pe, y_ok = sem("w_pe"), sem("w_sb"), sem("y_pe"), sem("y_ok")
        quant_v, quant_p = sem("quant_v"), sem("quant_p")
        zt_pe, zt_sb, ffn_pe, ffn_y, ffn_b, ffn_sum = (sem(n) for n in ("zt_pe", "zt_sb", "ffn_pe", "ffn_y", "ffn_b", "ffn_sum"))
        stored = sem("stored")

        raw, tr = (slots[:, 2 * n:2 * n + 2, :, :, :].rearrange("p g h w s -> p (g h w s)").bitcast(F32) for n in range(2))
        u_raw = [raw[:, n * 1536:(n + 1) * 1536].rearrange("p (c x) -> p c x", c=C) for n in range(3)]
        v_raw = [raw[0:R, 4608 + n * D:4608 + (n + 1) * D] for n in range(3)]
        ou_raw = raw[:, 5376:5760].rearrange("p (c x) -> p c x", c=C)
        ov_raw = [raw[:, 5760:6016], raw[0:R_OUT - P, 6016:6272]]
        wf_raw = raw[:, 6272:6528].bitcast(BF16).rearrange("p (c n) -> p c n", c=C)
        ut = tr[0:R, 0:4096].rearrange("p (h c d) -> p h c d", h=H, c=C)
        out_t = [tr[:, 4096:4352], tr[0:R_OUT - P, 4352:4608]]
        q_v = hid[:, 0:2, :].rearrange("p a b -> p (a b)")
        q_m = hid[:, 2:4, :].rearrange("p a b -> p (a b)")
        q_t = hid[:, 4:6, :].rearrange("p a b -> p (a b)")
        q_n = hid[:, 6:8, :].rearrange("p a b -> p (a b)")

        flat = "p a b -> p (a b)"

        def need_first(eng, *events):
            values = [n if isinstance(n, int) else eng.to_reg(n) for _, n in events]
            eng.wait_ge(ones_ok, 3)
            for (s, _), n in zip(events, values):
                need(eng, s, n)

        def need(eng, s, n):
            if not isinstance(n, int) or n > 0:
                eng.wait_ge(s, n)

        def reader(stage, a):
            if stage in ("v", "fc2_u") and a[-1]:
                return None
            return {
                "x1_t": lambda: (x1t_sb, 4, 2 * a[0] + a[1]),
                "qk": lambda: (qk_x, 8, a[0]),
                "v": lambda: (v_sb, 4, a[0]),
                "max_rows": lambda: (mt_sb, 4, a[0]),
                "out_norm": lambda: (ctx_ok, 8, 2 * a[0] + a[1]),
                "ctx_t": lambda: (ct_sb, 4, 2 * a[0] + a[1]),
                "out_proj": lambda: (h_ok, 4, 2 * a[0] + a[1]),
                "x2_t": lambda: (x2t_sb, 4, 2 * a[0] + a[1]),
                "fc1_u": lambda: (u_sb, 2, a[0]),
                "fc1_v": lambda: (hid_raw, 16, F * a[0] + a[1]),
                "fc2_u": lambda: (w_sb, 2, a[0]),
                "fc2_v": lambda: (y_ok, 4, 2 * a[0] + a[1]),
                "zq_t": lambda: (zt_sb, 4, 2 * a[0] + a[1]),
                "ffn": lambda: (ffn_y, 4, 2 * a[0] + a[1]),
            }.get(stage, lambda: None)()

        uses = [n for n, (_, stage, a) in enumerate(SCHED) if reader(stage, a)]
        assert NU == NST * HG and len(uses) % 2 == 0 and all(SCHED[n][0] >= 0 for n in uses[-2:])
        bank_of, using = {}, {}
        for n, (db, stage, a) in enumerate(SCHED):
            base = stage.removesuffix(".out")
            if n in uses:
                using[base] = uses.index(n) % 2
            if reader(base, a) or (base in ("v", "fc2_u")):
                bank_of[n] = using[base]

        def runs(s, n):
            return not isinstance(s, int) or 0 <= s + SCHED[n][0] < B

        def x_read(s, n):
            same = [m for m in uses if bank_of[m] == bank_of[n]]
            for back, places in ((0, [m for m in same if m < n]), (1, same), (2, same)):
                before = s - back
                valid = [m for m in places if runs(before, m)]
                if valid:
                    db, stage, a = SCHED[valid[-1]]
                    who, per, k = reader(stage, a)
                    return who, (before + db) * per + k + 1
            return None

        def run_steps(eng, stages):
            def step(s):
                for n, (db, stage, a) in enumerate(SCHED):
                    if stage in stages and runs(s, n):
                        if n in bank_of:
                            stages[stage]((s, n), s + db, *a)
                        else:
                            stages[stage](s + db, *a)
            step(-1)
            step(0)
            step(1)
            with eng.Fori(2, B - 1) as s:
                step(s)
            step(B - 1)
            step(B)

        def st_width(st):
            c, j = STEPS[st]
            return c, j, max(0, P * (j - TH * c))

        block = ctx.enter_context(nc.Block())

        @block.sync
        def _(sp):
            for name, k, u, v in (("q_in", 0, q_U, q_V), ("k_in", 1, k_U, k_V), ("v_in", 2, v_U, v_V)):
                sp.dma_start(u_raw[k], u.rearrange("(c p) h r -> p c (h r)", p=P)).then_inc(loaded[name], 16)
                sp.dma_start(v_raw[k].rearrange("r (h e) -> r h e", h=H), v.rearrange("h r e -> r h e")).then_inc(loaded[name], 16)
            sp.dma_start(ou_raw, out_U.rearrange("(c p) r -> p c r", p=P)).then_inc(loaded["out_in"], 16)
            sp.dma_start(ov_raw[0], out_V[0:P, :]).then_inc(loaded["out_in"], 16)
            sp.dma_start(ov_raw[1], out_V[P:R_OUT, :]).then_inc(loaded["out_in"], 16)
            for dst, src in (
                (g1, ln1_g.rearrange("(c p) -> p c", p=P)), (b1, ln1_b.rearrange("(c p) -> p c", p=P)),
                (g2, ln2_g.rearrange("(c p) -> p c", p=P)), (bb2, ln2_b.rearrange("(c p) -> p c", p=P)),
                (qb, q_b.rearrange("(f h) e -> (h e) f", f=2)), (kb, k_b.rearrange("(f h) e -> (h e) f", f=2)),
                (fc1b, fc1_b.rearrange("(f p) -> p f", p=P)),
                (vb, v_b.rearrange("h e -> (h e)").partition_broadcast(P)),
                (ob, out_b.partition_broadcast(P)), (b2, fc2_b.partition_broadcast(P)),
                (fb, ffn_bias.partition_broadcast(P)),
                (sc[:, 0:1], in_scale.partition_broadcast(P)), (sc[:, 1:2], w_scale.partition_broadcast(P)),
                (w1u, fc1_U.rearrange("(c p) r -> p c r", p=P)), (w1v, fc1_V),
                (w2u, fc2_U.rearrange("(f p) r -> p f r", p=P)), (w2v, fc2_V),
                (wf_raw, ffn_w.rearrange("(c p) n -> p c n", p=P)),
            ):
                with nc.allow_non_contiguous_dma(reason="a few short vectors, one element per partition"):
                    sp.dma_start(dst if isinstance(dst, bass.AP) else dst[:], src).then_inc(loaded["rest_in"], 16)

            def load_x(b, hf):
                need_first(sp, (x1t_pe, b * 4 + 2 * hf))
                sp.dma_start(x_in[:, :, :], hidden[b, hf * HALF:(hf + 1) * HALF, :].rearrange("(t p) d -> p t d", p=P)).then_inc(x_loaded, 16)

            def load_res(b, hf):
                need_first(sp, (y_ok, b * 4 + 2 * hf))
                sp.dma_start(x_res[:, :, :], hidden[b, hf * HALF:(hf + 1) * HALF, :].rearrange("(t p) d -> p t d", p=P)).then_inc(res_loaded, 16)

            def place(b, g):
                done = b * 8 + 4 * (g // 2) + 4
                need_first(sp, (qk_lo, done), (qk_mid, done), (qk_hi, done),
                           (scores_pe, (b - 1) * G * NST * HG + (g + 1) * NST * HG))
                sp.wait_ge(fold_sb, 7)
                sp.wait_ge(wf_ok, 7)
                both = parts[:, :, :, :].rearrange("p w n s -> p (w n) s")
                for hh in range(HG):
                    lo = (g % 2 * HG + hh) * DH
                    for r in range(SPLIT):
                        qp, kp = Q_PARTS[r], 3 + K_PARTS[r]
                        sp.dma_start(slots[DH * r:DH * (r + 1), g, hh, :, :],
                                     both[lo:lo + DH, qp:kp + 1:kp - qp, :]).then_inc(placed[g], 16)

            def max_rows(xn, b, g):
                need(sp, mt_sb, b * G + g + 1)
                for hh in range(HG):
                    sp.dma_start(qs[KS:KM, g, hh, :], m_rows[MROWS * hh:MROWS * (hh + 1), :]).then_inc(m_placed, 16)

            def store(b, hf):
                need_first(sp, (ln[4]["norm"], b * 8 + 4 * hf + 4))
                sp.dma_start(out[b, hf * HALF:(hf + 1) * HALF, :].rearrange("(t p) d -> p t d", p=P), h_sb[:, :, :]).then_inc(stored, 16)

            run_steps(sp, {"load_x": load_x, "load_res": load_res, "place": place, "max_rows.out": max_rows, "store": store})
            sp.wait_ge(stored, 2 * B * 16)

        @block.gpsimd
        def _(pool):
            pool.memset(ident[:, :], 0.0).then_inc(ident_ok, 1)
            pool.memset(ident_b[:, :], 0.0).then_inc(ident_ok, 1)
            pool.wait_ge(ident_ok, 2)
            for m in (ident, ident_b):
                pool.affine_select(out=m[:, :], in_=m[:, :], compare_op=ALU.not_equal, fill=1.0, base=0,
                                   pattern=[[-1, P]], channel_multiplier=1).then_inc(ident_ok, 1)
            pool.memset(mask[:, :], 0.0).then_inc(mask_ok, 1)
            pool.wait_ge(mask_ok, 1)
            pool.affine_select(out=mask[:, HALF - P:HALF], in_=mask[:, HALF - P:HALF], compare_op=ALU.is_ge, fill=NEG,
                               base=0, pattern=[[-1, P]], channel_multiplier=1).then_inc(mask_ok, 1)
            pool.memset(mask_t[:, :], 0.0).then_inc(mask_ok, 1)
            pool.wait_ge(mask_ok, 3)
            pool.affine_select(out=mask_t[:, :], in_=mask_t[:, :], compare_op=ALU.is_ge, fill=NEG,
                               base=0, pattern=[[1, P]], channel_multiplier=-1).then_inc(mask_ok, 1)
            pool.memset(half_neg[:, :], -0.5).then_inc(ones_ok, 1)
            pool.memset(vs[:, :, :, DH:DH + 1], 1.0).then_inc(ones_ok, 1)

            def power(n):
                def f(b, hf):
                    need(pool, ln[n]["norm"], b * 8 + 4 * hf)
                    need(pool, ln[n]["var"], b * 2 + hf + 1)
                    pool.tensor_tensor(rstd[n][:, :], var_eps[n][:, :], half_neg[:, :], ALU.pow).then_inc(ln[n]["rstd"], 1)
                return f

            def qk(xn, b, n):
                w, hf = n % 4 // 2, n % 2
                cols = slice(hf * HALF, (hf + 1) * HALF)
                need(pool, qk_x, b * 8 + n + 1)
                need(pool, qk_lo, b * 8 + n)
                need(pool, qk_hi, b * 8 + n + 1)
                pool.tensor_tensor(qk_rest[:, :], qk_full[:, :], parts[:, w, 0, cols], ALU.subtract).then_inc(qk_r, 1)

            def qk_parts(b, n):
                w, hf = n % 4 // 2, n % 2
                cols = slice(hf * HALF, (hf + 1) * HALF)
                need(pool, qk_mid, b * 8 + n + 1)
                pool.tensor_tensor(parts[:, w, 2, cols], qk_rest[:, :], parts[:, w, 1, cols], ALU.subtract).then_inc(qk_lo, 1)

            def add_biases(b, hf):
                need(pool, res_loaded, (b * 2 + hf + 1) * 16)
                need(pool, stored, (b * 2 + hf) * 16)
                need(pool, loaded["rest_in"], 18 * 16)
                for t in range(TH):
                    pool.tensor_tensor(h_sb[:, t, :], x_res[:, t, :], ob[:, :], ALU.add).then_inc(res_ob, 1)
                need(pool, res_ob, (b * 2 + hf + 1) * TH)
                for t in range(TH):
                    pool.tensor_tensor(x_res[:, t, :], x_res[:, t, :], b2[:, :], ALU.add).then_inc(res_b2, 1)

            def fc1_u(xn, b, hf):
                need(pool, h_ok, b * 4 + 2 * hf + 2)
                need(pool, res_b2, (b * 2 + hf + 1) * TH)
                xr, hx = x_res[:, :, :].rearrange(flat), h_sb[:, :, :].rearrange(flat)
                pool.tensor_tensor(xr, xr, hx, ALU.add).then_inc(res_h, 1)

            def quant(b, hf, part):
                k = b * 2 + hf
                if part == 0:
                    return
                if part == 2:
                    need(pool, quant_v, k * 5 + 5)
                    need(pool, zt_pe, k * C)
                    pool.tensor_tensor(zq[:, :, :].rearrange(flat), q_t, q_n, ALU.add).then_inc(quant_p, 1)
                    return
                need(pool, quant_v, k * 5 + 4)
                pool.tensor_tensor(q_t, q_v, q_m, ALU.add).then_inc(quant_p, 1)
                need(pool, quant_p, k * 3 + 1)
                pool.tensor_tensor(q_t, q_t, q_m, ALU.subtract).then_inc(quant_p, 1)

            def ffn(xn, b, hf, pr):
                k = b * 4 + 2 * hf + pr
                need(pool, ffn_y, k + 1)
                pair = slice(2 * pr, 2 * pr + 2)
                for t in (2 * pr, 2 * pr + 1):
                    pool.tensor_tensor(yb[:, t, :], yb[:, t, :], fb[:, :], ALU.add).then_inc(ffn_b, 1)
                need(pool, ffn_b, k * 2 + 2)
                pool.tensor_tensor(h_sb[:, pair, :].rearrange(flat), x2[:, pair, :].rearrange(flat),
                                   yb[:, pair, :].rearrange(flat), ALU.add).then_inc(ffn_sum, 1)

            run_steps(pool, {"ln1_aggr": power(1), "ln2_aggr": power(2), "ln3_aggr": power(3), "ln4_aggr": power(4),
                             "qk.out": qk, "qk_parts": qk_parts, "add_biases": add_biases, "fc1_u.out": fc1_u,
                             "quant": quant, "ffn.out": ffn})

        @block.scalar
        def _(act):
            act.wait_ge(loaded["rest_in"], 18 * 16)

            def x1_t(xn, b, hf, ch):
                need(act, x1t_pe, b * 4 + 2 * hf + ch + 1)
                need(act, v_pe, b * 4)
                need(act, qk_pe, b * 8)
                act.activation(x1t[:, ch, hf * HALF:(hf + 1) * HALF], px[bank_of[xn[1]]][:, :], ACT.Identity,
                               bias=b1[:, ch:ch + 1], scale=g1[:, ch:ch + 1]).then_inc(x1t_sb, 1)

            def qk(xn, b, n):
                f, w, hf = n // 4, n % 4 // 2, n % 2
                cols = slice(hf * HALF, (hf + 1) * HALF)
                bias = (qb, kb)[w][:, f:f + 1]
                need(act, qk_pe, b * 8 + n + 1)
                for g in range(G):
                    if g // 2 != f:
                        need(act, placed[g], (b if f else b) * 16 * HG * SPLIT if not f else (b + 1) * 16 * HG * SPLIT)
                act.activation(parts[:, w, 0, cols], px[bank_of[xn[1]]][:, :], ACT.Identity, bias=bias).then_inc(qk_hi, 1)
                need(act, qk_r, b * 8 + n)
                act.activation(qk_full[:, :], px[bank_of[xn[1]]][:, :], ACT.Identity, bias=bias).then_inc(qk_x, 1)

            def max_rows(xn, b, g):
                need(act, mt_pe, b * 4 + g + 1)
                need(act, m_placed, (b * 4 + g) * HG * 16)
                act.activation(m_rows[:, :], px[bank_of[xn[1]]][0:MROWS * HG, :].bitcast(BF16), ACT.Copy).then_inc(mt_sb, 1)

            def scores(b, g, st, hh):
                c, j, lo = st_width(st)
                step = g * NST + st
                n = step * HG + hh
                need(act, scores_pe, b * G * NST * HG + n + 1)
                need(act, pv_pe, b * G * NST + step - NPT + 1)
                act.activation(probs[:, step % NPT, hh, lo:HALF], ps[n % S_RING][:, lo:HALF], ACT.Exp,
                               scale=SCALE).then_inc(exp_done, 1)

            def out_copy(b, g, c):
                k = 2 * g + c
                need(act, pv_pe, b * G * NST + g * NST + (NST if c else TH))
                need(act, o_t, b * 8 + k)
                act.activation(o_sb[:, :], po[:, :], ACT.Copy).then_inc(o_copied, 1)

            def ctx_tr(xn, b, hf, ch):
                need(act, ct_pe, b * 4 + 2 * hf + ch + 1)
                need(act, op_pe, b * 4)
                act.activation(ctx_t[:, hf, ch, :], px[bank_of[xn[1]]][:, :], ACT.Copy).then_inc(ct_sb, 1)

            def x2_t(xn, b, hf, ch):
                need(act, x2t_pe, b * 4 + 2 * hf + ch + 1)
                need(act, u_pe, b * 2 + hf)
                act.activation(x2t[:, ch, :], px[bank_of[xn[1]]][:, :], ACT.Identity,
                               bias=bb2[:, ch:ch + 1], scale=g2[:, ch:ch + 1]).then_inc(x2t_sb, 1)

            def fc1_u(xn, b, hf):
                need(act, u_pe, b * 2 + hf + 1)
                need(act, hid_pe, (b * 2 + hf) * F)
                act.activation(u_t[:, :], px[bank_of[xn[1]]][:, :], ACT.Copy).then_inc(u_sb, 1)

            def gelu(b, hf):
                need(act, hid_raw, (b * 2 + hf + 1) * F)
                act.activation(hid[:, :, :].rearrange(flat), hid[:, :, :].rearrange(flat), ACT.Gelu_apprx_tanh).then_inc(hid_ok, 1)

            def fc2_u(xn, b, hf):
                need(act, w_pe, b * 2 + hf + 1)
                need(act, y_pe, (b * 2 + hf) * 2)
                act.activation(w_t[:, :], px[bank_of[xn[1]]][:, :], ACT.Copy).then_inc(w_sb, 1)

            def zq_t(xn, b, hf, ch):
                need(act, zt_pe, b * 4 + 2 * hf + ch + 1)
                need(act, ffn_pe, (b * 2 + hf) * 2)
                act.activation(zqt[:, ch, :], px[bank_of[xn[1]]][:, 0:HALF // 2].bitcast(BF16), ACT.Copy).then_inc(zt_sb, 1)

            def ffn(xn, b, hf, pr):
                k = b * 4 + 2 * hf + pr
                need(act, ffn_pe, k + 1)
                act.wait_ge(scale_ok, 3)
                act.activation(yb[:, 2 * pr:2 * pr + 2, :].rearrange(flat), px[bank_of[xn[1]]][:, :], ACT.Copy,
                               scale=sc[:, 4:5]).then_inc(ffn_y, 1)

            run_steps(act, {"x1_t.out": x1_t, "qk.out": qk, "max_rows.out": max_rows, "scores": scores,
                            "out_copy": out_copy, "ctx_t.out": ctx_tr, "x2_t.out": x2_t, "fc1_u.out": fc1_u,
                            "gelu": gelu, "fc2_u.out": fc2_u, "zq_t.out": zq_t, "ffn.out": ffn})

        @block.tensor
        def _(pe):
            pe.wait_ge(ident_ok, 4)
            for w, name in enumerate(("q_in", "k_in", "v_in")):
                pe.wait_ge(loaded[name], 32)
                for h2 in range(H // 2):
                    n = w * (H // 2) + h2
                    if n >= 4:
                        pe.wait_ge(ut_sb, n - 3)
                    for hl in range(2):
                        for c in range(C):
                            k = 2 * hl + c
                            last = pe.transpose(bank[n % 4][0:R, k * P:(k + 1) * P],
                                                u_raw[w][:, c, (2 * h2 + hl) * R:(2 * h2 + hl + 1) * R], ident[:, :])
                    last.then_inc(ut_pe, 1)
                pe.wait_ge(ut_sb, (w + 1) * (H // 2))
                if w >= 2:
                    pe.wait_ge(fold_sb, w - 1)
                for c in range(C):
                    for h in range(H):
                        last = pe.matmul(bank[4 + w % 2][:, c * D + h * DH:c * D + (h + 1) * DH], ut[:, h, c, :],
                                         v_raw[w][:, h * DH:(h + 1) * DH], start=True, stop=True)
                last.then_inc(fold_pe, 1)
            pe.wait_ge(loaded["out_in"], 48)
            for c in range(C):
                pe.transpose(bank[6][:, c * P:(c + 1) * P], ou_raw[:, c, 0:P], ident[:, :])
                last = pe.transpose(bank[7][0:R_OUT - P, c * P:(c + 1) * P], ou_raw[:, c, P:R_OUT], ident[:, :])
            last.then_inc(fold_pe, 1)
            pe.wait_ge(fold_sb, 5)
            for c in range(C):
                pe.matmul(bank[5][:, c * D:(c + 1) * D], out_t[0][:, c * P:(c + 1) * P], ov_raw[0], start=True, stop=False)
                last = pe.matmul(bank[5][:, c * D:(c + 1) * D], out_t[1][:, c * P:(c + 1) * P], ov_raw[1], start=False, stop=True)
            last.then_inc(fold_pe, 1)
            pe.wait_ge(fold_sb, 6)
            pe.wait_ge(loaded["rest_in"], 18 * 16)
            pe.wait_ge(ones_ok, 3)
            pe.wait_ge(mask_ok, 4)

            def x_bank(xn):
                free = x_read(*xn)
                if free:
                    need(pe, *free)
                return px[bank_of[xn[1]]]

            def turn(x, src, s, idn):
                for t in range(TH):
                    last = pe.transpose(x[:, t * P:(t + 1) * P], src(t), idn[:, :])
                last.then_inc(s, 1)

            def x1_t(xn, b, hf, ch):
                x = x_bank(xn)
                need(pe, ln[1]["norm"], b * 8 + 4 * hf + 4)
                turn(x, lambda t: x_in[:, t, ch * P:(ch + 1) * P], x1t_pe, ident)

            def qk(xn, b, n):
                x = x_bank(xn)
                f, w, hf = n // 4, n % 4 // 2, n % 2
                need(pe, x1t_sb, b * 4 + 2 * hf + 2)
                for ch in range(C):
                    last = pe.matmul(x[:, :], (wq, wk)[w][:, ch, f * P:(f + 1) * P], x1t[:, ch, hf * HALF:(hf + 1) * HALF],
                                     start=(ch == 0), stop=(ch == C - 1))
                last.then_inc(qk_pe, 1)

            def v(xn, b, g, part):
                x = px[bank_of[xn[1]]] if part else x_bank(xn)
                need(pe, x1t_sb, b * 4 + 4)
                gd = HG * DH
                for t in range(TH * part, TH * (part + 1)):
                    for ch in range(C):
                        last = pe.matmul(x[:, t * gd:(t + 1) * gd], x1t[:, ch, t * P:(t + 1) * P],
                                         wv[:, ch, g * gd:(g + 1) * gd], start=(ch == 0), stop=(ch == C - 1))
                if part:
                    last.then_inc(v_pe, 1)

            def row_max_(b, g, u):
                hh, i, part = UNITS[u]
                n = g * NU + u
                if u == 0:
                    need(pe, placed[g], (b + 1) * 16 * HG * SPLIT)
                need(pe, row_max, b * G * NU + n - A_RING + 1)
                k1 = min((i + 1) * P, (part + 1) * HALF)
                pe.matmul(pa[n % A_RING][:, 0:k1 - part * HALF], qs[0:KS, g, hh, i * P:(i + 1) * P],
                          ks[0:KS, g, hh, part * HALF:k1], start=True, stop=True).then_inc(max_scores, 1)

            def max_rows(xn, b, g):
                x = x_bank(xn)[0:MROWS * HG, :].bitcast(BF16)
                need(pe, neg_max, (b * 4 + g + 1) * 5)
                for i in range(T):
                    last = pe.transpose(x[:, i * P:(i + 1) * P], m_part[:, i, :, :].rearrange(flat), ident_b[:, :])
                last.then_inc(mt_pe, 1)

            def scores(b, g, st, hh):
                c, j, lo = st_width(st)
                n = (g * NST + st) * HG + hh
                if st == 0 and hh == 0:
                    need(pe, m_placed, (b * 4 + g + 1) * HG * 16)
                need(pe, exp_done, b * G * NST * HG + n - S_RING + 1)
                last = pe.matmul(ps[n % S_RING][:, lo:HALF], ks[0:KM, g, hh, j * P:(j + 1) * P],
                                 qs[0:KM, g, hh, c * HALF + lo:(c + 1) * HALF], start=True, stop=st not in DIAG)
                if st in DIAG:
                    last = pe.matmul(ps[n % S_RING][:, lo:lo + P], ident_b[:, :], mask_t[:, :], start=False, stop=True)
                last.then_inc(scores_pe, 1)

            def values(b, g, st):
                c, j, lo = st_width(st)
                step = g * NST + st
                if st == 0:
                    need(pe, v_sb, b * 4 + g + 1)
                if j == 0:
                    need(pe, o_copied, b * 8 + 2 * g + c)
                need(pe, exp_done, (b * G * NST + step) * HG + HG)
                for hh in range(HG):
                    last = pe.matmul(po[32 * hh:32 * hh + DH + 1, lo:HALF], vs[:, j, g * HG + hh, :],
                                     probs[:, step % NPT, hh, lo:HALF], start=(j == 0), stop=(j == TH * (c + 1) - 1))
                last.then_inc(pv_pe, 1)

            def out_norm(xn, b, g, c):
                x = x_bank(xn)
                need(pe, o_copied, b * 8 + 2 * g + c + 1)
                turn(x, lambda t: o_sb[:, t * P:(t + 1) * P], o_t, ident)

            def ctx_tr(xn, b, hf, ch):
                x = x_bank(xn)
                need(pe, ctx_ok, b * 8 + 2 * (G - 1) + hf + 1)
                turn(x, lambda t: ctx_sb[:, TH * hf + t, ch * P:(ch + 1) * P], ct_pe, ident)

            def out_proj(xn, b, hf, pr):
                x = x_bank(xn)
                need(pe, ct_sb, b * 4 + 2 * hf + 2)
                for tt in range(2):
                    for ch in range(C):
                        t = 2 * pr + tt
                        last = pe.matmul(x[:, tt * D:(tt + 1) * D], ctx_t[:, hf, ch, t * P:(t + 1) * P], wo[:, ch, :],
                                         start=(ch == 0), stop=(ch == C - 1))
                last.then_inc(op_pe, 1)

            def x2_t(xn, b, hf, ch):
                x = x_bank(xn)
                need(pe, ln[2]["norm"], b * 8 + 4 * hf + 4)
                turn(x, lambda t: x2[:, t, ch * P:(ch + 1) * P], x2t_pe, ident)

            def fc1_u(xn, b, hf):
                x = x_bank(xn)
                need(pe, x2t_sb, b * 4 + 2 * hf + 2)
                for ch in range(C):
                    last = pe.matmul(x[:, :], w1u[:, ch, :], x2t[:, ch, :], start=(ch == 0), stop=(ch == C - 1))
                last.then_inc(u_pe, 1)

            def fc1_v(xn, b, hf, f):
                x = x_bank(xn)
                need(pe, u_sb, b * 2 + hf + 1)
                pe.matmul(x[:, :], w1v[:, f * P:(f + 1) * P], u_t[:, :], start=True, stop=True).then_inc(hid_pe, 1)

            def fc2_u(xn, b, hf, part):
                x = px[bank_of[xn[1]]] if part else x_bank(xn)
                need(pe, hid_ok, b * 2 + hf + 1)
                for f in range(2 * part, 2 * part + 2):
                    last = pe.matmul(x[:, :], w2u[:, f, :], hid[:, f, :], start=(f == 0), stop=(f == F - 1))
                if part == F // 2 - 1:
                    last.then_inc(w_pe, 1)

            def fc2_v(xn, b, hf, pr):
                x = x_bank(xn)
                need(pe, w_sb, b * 2 + hf + 1)
                for tt in range(2):
                    t = 2 * pr + tt
                    last = pe.matmul(x[:, tt * D:(tt + 1) * D], w_t[:, t * P:(t + 1) * P], w2v[:, :], start=True, stop=True)
                last.then_inc(y_pe, 1)

            def zq_t(xn, b, hf, ch):
                x = x_bank(xn)[:, 0:HALF // 2].bitcast(BF16)
                need(pe, quant_p, (b * 2 + hf + 1) * 3)
                turn(x, lambda t: zq[:, t, ch * P:(ch + 1) * P], zt_pe, ident_b)

            def ffn(xn, b, hf, pr):
                x = x_bank(xn)
                pe.wait_ge(wf_ok, 7)
                need(pe, zt_sb, b * 4 + 2 * hf + 2)
                for tt in range(2):
                    t = 2 * pr + tt
                    for ch in range(C):
                        last = pe.matmul(x[:, tt * D:(tt + 1) * D], zqt[:, ch, t * P:(t + 1) * P], wf[:, ch, :],
                                         start=(ch == 0), stop=(ch == C - 1))
                last.then_inc(ffn_pe, 1)

            run_steps(pe, {"x1_t": x1_t, "qk": qk, "v": v, "row_max": row_max_, "max_rows": max_rows, "scores": scores,
                           "values": values, "out_norm": out_norm, "ctx_t": ctx_tr, "out_proj": out_proj, "x2_t": x2_t,
                           "fc1_u": fc1_u, "fc1_v": fc1_v, "fc2_u": fc2_u, "fc2_v": fc2_v, "zq_t": zq_t, "ffn": ffn})

        @block.vector
        def _(dve):
            dve.memset(po[:, :], 0.0).then_inc(fold_sb, 1)
            for w in range(3):
                for h2 in range(H // 2):
                    n = w * (H // 2) + h2
                    dve.wait_ge(ut_pe, n + 1)
                    if h2 == 0 and w:
                        dve.wait_ge(fold_pe, w)
                    dve.tensor_copy(ut[:, 2 * h2:2 * h2 + 2, :, :].rearrange("p h c d -> p (h c d)"),
                                    bank[n % 4][0:R, :]).then_inc(ut_sb, 1)
                dve.wait_ge(fold_pe, w + 1)
                dve.tensor_copy((wq, wk, wv)[w][:, :, :].rearrange(flat), bank[4 + w % 2][:, :]).then_inc(fold_sb, 1)
            dve.wait_ge(fold_pe, 4)
            dve.tensor_copy(out_t[0], bank[6][:, 0:D])
            dve.tensor_copy(out_t[1], bank[7][0:R_OUT - P, 0:D]).then_inc(fold_sb, 1)
            dve.wait_ge(fold_pe, 5)
            dve.tensor_copy(wo[:, :, :].rearrange(flat), bank[5][:, :]).then_inc(fold_sb, 1)
            dve.wait_ge(fold_sb, 6)
            dve.memset(po[:, :], 0.0).then_inc(fold_sb, 1)
            dve.wait_ge(loaded["rest_in"], 18 * 16)
            dve.reciprocal(sc[:, 2:3], sc[:, 0:1]).then_inc(scale_ok, 1)
            dve.reciprocal(sc[:, 3:4], sc[:, 1:2]).then_inc(scale_ok, 1)
            dve.tensor_tensor(sc[:, 4:5], sc[:, 0:1], sc[:, 1:2], ALU.mult).then_inc(scale_ok, 1)
            dve.wait_ge(scale_ok, 3)
            wv_, wm, wt, wn = (a[:, 0:C * D] for a in (q_v, q_m, q_t, q_n))
            dve.tensor_scalar(wv_, wf_raw[:, :, :].rearrange(flat), sc[:, 3:4], None, ALU.mult).then_inc(wf_ok, 1)
            dve.wait_ge(wf_ok, 1)
            dve.tensor_scalar(wm.bitcast(U32), wv_.bitcast(U32), 0x7F800000, None, ALU.bitwise_and).then_inc(wf_ok, 1)
            dve.wait_ge(wf_ok, 2)
            dve.tensor_scalar(wm, wm, 2.0 ** -6, 1.5 * 2.0 ** 20, ALU.max, ALU.mult).then_inc(wf_ok, 1)
            dve.wait_ge(wf_ok, 3)
            dve.tensor_tensor(wt, wv_, wm, ALU.add).then_inc(wf_ok, 1)
            dve.wait_ge(wf_ok, 4)
            dve.tensor_tensor(wt, wt, wm, ALU.subtract).then_inc(wf_ok, 1)
            dve.wait_ge(wf_ok, 5)
            dve.tensor_scalar(wn, wt, 7.4e35, 0.0, ALU.mult, ALU.mult).then_inc(wf_ok, 1)
            dve.wait_ge(wf_ok, 6)
            dve.tensor_tensor(wf[:, :, :].rearrange(flat), wt, wn, ALU.add).then_inc(wf_ok, 1)
            dve.wait_ge(wf_ok, 7)
            dve.memset(ks[KS:KM, :, :, :].bitcast(F32), float(np.uint32(0x3F803F80).view(np.float32))).then_inc(ones_ok, 1)

            def stats(n, buf, ready):
                def f(b, hf, t0):
                    k = b * 2 + hf
                    if t0 == 0:
                        need(dve, *ready(b, hf))
                        need(dve, ln[n]["aggr"], k * TH)
                    for t in (t0, t0 + 1):
                        dve.bn_stats(st6[n][:, t, :], buf[:, t, :]).then_inc(ln[n]["stats"], 1)
                return f

            def aggr(n):
                def f(b, hf):
                    s = ln[n]
                    k = b * 2 + hf
                    need_first(dve, (s["stats"], (k + 1) * TH), (s["norm"], k * TH), (s["var"], k))
                    for t in range(TH):
                        dve.bn_aggr(mv[n][:, t, :], st6[n][:, t, :]).then_inc(s["aggr"], 1)
                    need(dve, s["aggr"], (k + 1) * TH)
                    need(dve, s["rstd"], k)
                    dve.tensor_scalar(var_eps[n][:, :], mv[n][:, :, 1], EPS, None, ALU.add).then_inc(s["var"], 1)
                return f

            def apply(n, src, dst, free):
                def f(b, hf, t0):
                    s = ln[n]
                    if t0 == 0:
                        need(dve, s["rstd"], b * 2 + hf + 1)
                        if free:
                            need(dve, *free(b, hf))
                    for t in (t0, t0 + 1):
                        dve.tensor_scalar(dst[:, t, :], src[:, t, :], mv[n][:, t, 0:1], rstd[n][:, t:t + 1],
                                          ALU.subtract, ALU.mult).then_inc(s["norm"], 1)
                return f

            def qk_parts(b, n):
                w, hf = n % 4 // 2, n % 2
                need(dve, qk_r, b * 8 + n + 1)
                dve.tensor_copy(parts[:, w, 1, hf * HALF:(hf + 1) * HALF], qk_rest[:, :]).then_inc(qk_mid, 1)

            def v(xn, b, g):
                need(dve, v_pe, b * 4 + g + 1)
                need(dve, pv_pe, (b - 1) * G * NST + (g + 1) * NST)
                gd = HG * DH
                x = px[bank_of[xn[1]]]
                for t in range(T):
                    last = dve.tensor_tensor(vs[:, t, g * HG:(g + 1) * HG, 0:DH],
                                             x[:, t * gd:(t + 1) * gd].rearrange("p (h e) -> p h e", h=HG),
                                             vb[:, g * gd:(g + 1) * gd].rearrange("p (h e) -> p h e", h=HG), ALU.add)
                last.then_inc(v_sb, 1)

            def row_max_(b, g, u):
                hh, i, part = UNITS[u]
                n = g * NU + u
                k = b * G * NU + n
                if u == 0:
                    need(dve, neg_max, (b * 4 + g) * 5)
                need(dve, row_max, k - TRASH + 1)
                need_first(dve, (max_scores, k + 1))
                dst = (mx_hi[:, i - TH, hh:hh + 1] if part else mx[:, i, hh:hh + 1])
                if i >= TH and part == 0:
                    dve.tensor_reduce(dst, pa[n % A_RING][:, :], AX.X, ALU.max).then_inc(row_max, 1)
                else:
                    w = (i + 1) * P - part * HALF
                    dve.tensor_tensor_reduce(trash[:, n % TRASH, 0:w], pa[n % A_RING][:, 0:w], mask[:, HALF - w:HALF],
                                             1.0, 3.0 * NEG, ALU.add, ALU.max, dst).then_inc(row_max, 1)

            def max_parts(b, g):
                k = (b * 4 + g) * 5
                need(dve, row_max, (b * G + g + 1) * NU)
                dve.tensor_tensor(mx[:, TH:T, :], mx[:, TH:T, :], mx_hi[:, :, :], ALU.max).then_inc(neg_max, 1)
                need(dve, neg_max, k + 1)
                need(dve, mt_pe, b * 4 + g)
                dve.tensor_scalar(m_part[:, :, :, 0], mx[:, :, :], -1.0, None, ALU.mult).then_inc(neg_max, 1)
                need(dve, neg_max, k + 2)
                dve.scalar_tensor_tensor(out=m_rest[:, :, :], in0=mx[:, :, :], scalar=-1.0, in1=m_part[:, :, :, 0],
                                         op0=ALU.mult, op1=ALU.subtract).then_inc(neg_max, 1)
                need(dve, neg_max, k + 3)
                dve.tensor_copy(m_part[:, :, :, 1], m_rest[:, :, :]).then_inc(neg_max, 1)
                need(dve, neg_max, k + 4)
                dve.tensor_tensor(m_part[:, :, :, 2], m_rest[:, :, :], m_part[:, :, :, 1], ALU.subtract).then_inc(neg_max, 1)

            def out_norm(xn, b, g, c):
                k = b * 8 + 2 * g + c
                x = px[bank_of[xn[1]]][:, :].rearrange("p (t h e) -> p t h e", t=TH, h=HG)
                need(dve, o_t, k + 1)
                need(dve, ctx_ok, k)
                dve.reciprocal(rden[:, :, :, :], x[:, :, :, DH:DH + 1]).then_inc(o_rden, 1)
                need(dve, o_rden, k + 1)
                need(dve, ct_pe, (b - 1) * 4 + 2 * c + 2)
                dst = ctx_sb[:, TH * c:TH * (c + 1), g * HG * DH:(g + 1) * HG * DH].rearrange("p t (h e) -> p t h e", h=HG)
                dve.tensor_tensor(dst, x[:, :, :, 0:DH], rden[:, :, :, :].to_broadcast([P, TH, HG, DH]),
                                  ALU.mult).then_inc(ctx_ok, 1)

            def out_proj(xn, b, hf, pr):
                k = b * 4 + 2 * hf + pr
                need(dve, op_pe, k + 1)
                need(dve, res_ob, (b * 2 + hf + 1) * TH)
                dst = h_sb[:, 2 * pr:2 * pr + 2, :].rearrange(flat)
                dve.tensor_tensor(dst, px[bank_of[xn[1]]][:, :], dst, ALU.add).then_inc(h_ok, 1)

            def fc1_v(xn, b, hf, f):
                k = b * 2 + hf
                need(dve, hid_pe, k * F + f + 1)
                need(dve, w_pe, k)
                need(dve, quant_p, k * 3)
                dve.tensor_scalar(hid[:, f, :], px[bank_of[xn[1]]][:, :], fc1b[:, f:f + 1], None, ALU.add).then_inc(hid_raw, 1)

            def fc2_v(xn, b, hf, pr):
                need(dve, y_pe, b * 4 + 2 * hf + pr + 1)
                need(dve, res_h, b * 2 + hf + 1)
                pair = slice(2 * pr, 2 * pr + 2)
                dve.tensor_tensor(h_sb[:, pair, :].rearrange(flat), px[bank_of[xn[1]]][:, :],
                                  x_res[:, pair, :].rearrange(flat), ALU.add).then_inc(y_ok, 1)

            def quant(b, hf, part):
                k = (b * 2 + hf) * 5
                if part == 0:
                    need(dve, ln[3]["norm"], (b * 2 + hf + 1) * TH)
                    need(dve, w_pe, b * 2 + hf + 1)
                    need(dve, ffn_sum, (b * 2 + hf) * 2)
                    z16 = yb[:, :, :].rearrange(flat)
                    dve.tensor_copy(z16, x2[:, :, :].rearrange(flat)).then_inc(quant_v, 1)
                    need(dve, quant_v, k + 1)
                    dve.tensor_scalar(q_v, z16, sc[:, 2:3], None, ALU.mult).then_inc(quant_v, 1)
                elif part == 1:
                    need(dve, quant_v, k + 2)
                    dve.tensor_scalar(q_m.bitcast(U32), q_v.bitcast(U32), 0x7F800000, None, ALU.bitwise_and).then_inc(quant_v, 1)
                    need(dve, quant_v, k + 3)
                    dve.tensor_scalar(q_m, q_m, 2.0 ** -6, 1.5 * 2.0 ** 20, ALU.max, ALU.mult).then_inc(quant_v, 1)
                else:
                    need(dve, quant_p, (b * 2 + hf) * 3 + 2)
                    dve.tensor_scalar(q_n, q_t, 7.4e35, 0.0, ALU.mult, ALU.mult).then_inc(quant_v, 1)

            run_steps(dve, {
                "ln1_stats": stats(1, x_in, lambda b, hf: (x_loaded, (b * 2 + hf + 1) * 16)),
                "ln1_aggr": aggr(1),
                "ln1_apply": apply(1, x_in, x_in, None),
                "ln2_stats": stats(2, h_sb, lambda b, hf: (h_ok, b * 4 + 2 * hf + 2)),
                "ln2_aggr": aggr(2),
                "ln2_apply": apply(2, h_sb, x2, lambda b, hf: (ffn_sum, (b * 2 + hf) * 2)),
                "ln3_stats": stats(3, h_sb, lambda b, hf: (y_ok, b * 4 + 2 * hf + 2)),
                "ln3_aggr": aggr(3),
                "ln3_apply": apply(3, h_sb, x2, lambda b, hf: (x2t_pe, b * 4 + 2 * hf + 2)),
                "ln4_stats": stats(4, h_sb, lambda b, hf: (ffn_sum, b * 4 + 2 * hf + 2)),
                "ln4_aggr": aggr(4),
                "ln4_apply": apply(4, h_sb, h_sb, None),
                "qk_parts": qk_parts, "v.out": v, "row_max": row_max_, "max_parts": max_parts,
                "out_norm.out": out_norm, "out_proj.out": out_proj, "fc1_v.out": fc1_v, "fc2_v.out": fc2_v,
                "quant": quant})


_INS = ["L0_attn_hidden_states", "L0_attn_ln1_g", "L0_attn_ln1_b", "L0_attn_ln2_g", "L0_attn_ln2_b",
        "L0_attn_q_U", "L0_attn_q_V", "L0_attn_q_b", "L0_attn_k_U", "L0_attn_k_V", "L0_attn_k_b",
        "L0_attn_v_U", "L0_attn_v_V", "L0_attn_v_b", "L0_attn_out_U", "L0_attn_out_V", "L0_attn_out_b",
        "L0_attn_fc1_U", "L0_attn_fc1_V", "L0_attn_fc1_b", "L0_attn_fc2_U", "L0_attn_fc2_V", "L0_attn_fc2_b",
        "L0_ffn_kernel", "L0_ffn_input_scale", "L0_ffn_kernel_scale", "L0_ffn_bias"]


def kernel(**inputs):
    import numpy as _np
    import concourse.bacc as _bacc
    from concourse import mybir as _mybir
    from concourse.bass_utils import run_bass_kernel_spmd as _run

    nc = _bacc.Bacc("TRN2", target_bir_lowering=False, num_devices=1)
    arrays, args = {}, []
    for name in _INS:
        a = _np.ascontiguousarray(inputs[name])
        arrays[f"in_{name}"] = a
        args.append(nc.dram_tensor(f"in_{name}", a.shape, _mybir.dt.from_np(a.dtype), kind="ExternalInput").ap())
    args.append(nc.dram_tensor("out_0", (B, S, D), _mybir.dt.float32, kind="ExternalOutput").ap())
    build(nc, *args)
    r = _run(nc, [arrays], core_ids=[0])
    return r.results[0]["out_0"]
```

```python
from contextlib import ExitStack

import numpy as np

import concourse.bass as bass
from concourse import mybir

ALU = mybir.AluOpType
ACT = mybir.ActivationFunctionType
AX = mybir.AxisListType
F32 = mybir.dt.float32
BF16 = mybir.dt.bfloat16
U32 = mybir.dt.uint32

P = 128
B, S, D = 8, 1024, 256
H, DH, R = 16, 16, 48
R_OUT, R_MLP, FF = 192, 128, 1024
T = S // P
C = D // P
HALF = S // 2
TH = T // 2
F = FF // P
G = 4
HG = H // G
SPLIT = 6
KS = SPLIT * DH
MROWS = 3
KM = KS + MROWS
Q_PARTS = (0, 0, 0, 1, 1, 2)
K_PARTS = (0, 1, 2, 0, 1, 0)
EPS = 1e-5
NEG = -1.0e30
SCALE = DH ** -0.5
GELU_1 = (2.0 / np.pi) ** 0.5
GELU_3 = 0.044715 * GELU_1

STEPS = [(c, j) for c in range(2) for j in range(TH * (c + 1))]
NST = len(STEPS)
UNITS = [(hh, i, part) for hh in range(HG) for i in range(T) for part in range(1 + (i >= TH))]
NU = len(UNITS)
A_RING, S_RING, NPT, TRASH = 3, 2, 2, 2
DIAG = [n for n, (c, j) in enumerate(STEPS) if j >= TH * c]

LAG_OUT, LAG_ROWS, LAG_LOAD, LAG_STORE, LAG_PLACE, LAG_BIASES = 1, 2, 6, 5, 14, 1
LAG_POWER, LAG_PARTS, LAG_TANH, LAG_GELU, LAG_QUANT, LAG_ZQ, LAG_SUM = 3, 2, 3, 5, 6, 5, 4
V_SLOTS = (68, 184, 186, 6)
LN1_SLOT, CTX_SLOT = 4, 4
GELU_SLOTS = 2
CAPACITY = 3

AFTER_BANKS = ("out_proj", "x2_t", "fc1_u", "fc1_v", "fc2_u", "fc2_v", "zq_t", "ffn")
AFTER = AFTER_BANKS + ("load_res", "add_biases", "gelu_mid", "gelu_tanh", "gelu", "quant", "store") + tuple(
    f"ln{n}_{part}" for n in (2, 3, 4) for part in ("stats", "aggr", "apply"))
LAST_LAG = 27


def schedule():
    slots = G * NST * HG
    block = NST * HG
    more = [[] for _ in range(slots)]
    bank_use = [None] * slots
    load = {e: [0] * slots for e in ("dve", "act")}

    def weight(stage):
        stage = stage.rstrip("01234").replace("ln1", "ln").replace("ln2", "ln").replace("ln3", "ln").replace("ln4", "ln")
        return {
            "x1_t.out": {"act": 2}, "qk.out": {"act": 2}, "max_rows.out": {"act": 2}, "ctx_t.out": {"act": 2},
            "x2_t.out": {"act": 2}, "fc1_u.out": {"act": 2}, "fc2_u.out": {"act": 2}, "zq_t.out": {"act": 2},
            "ffn.out": {"act": 2}, "gelu_tanh": {"act": 2}, "out_copy": {"act": 2},
            "fc1_v.out": {"act": 2, "dve": 1}, "gelu_mid": {"dve": 1}, "gelu": {"dve": 1}, "quant": {"dve": 2},
            "ln_stats": {"dve": 2}, "ln_aggr": {"dve": 1}, "ln_apply": {"dve": 2}, "qk_parts": {"dve": 1},
            "max_parts": {"dve": 2}, "v.out": {"dve": 2}, "out_norm.out": {"dve": 1}, "out_proj.out": {"dve": 2},
            "fc2_v.out": {"dve": 2},
        }.get(stage, {})

    def free(n, stage):
        return all(load[e][n] + w <= CAPACITY for e, w in weight(stage).items())

    def hold(n, stage):
        for e, w in weight(stage).items():
            load[e][n] += w

    def put(n, db, stage, *args):
        while not free(n, stage):
            n += 1
        more[n].append((db, stage, args))
        hold(n, stage)
        return n

    def put_x(n, db, stage, *args, parts=1):
        while any(bank_use[n:n + parts]) or not free(n + parts, stage + ".out"):
            n += 1
        for k in range(parts):
            bank_use[n + k] = (db, stage, args + ((k,) if parts > 1 else ()))
        return put(n + parts, db, stage + ".out", *args)

    def norm(n, db, which, hf):
        for t in range(0, TH, 2):
            n = put(n, db, f"ln{which}_stats", hf, t) + 1
        n = put(n, db, f"ln{which}_aggr", hf) + LAG_POWER
        for t in range(0, TH, 2):
            n = put(n, db, f"ln{which}_apply", hf, t) + 1
        return n

    def project(n, k):
        n = put_x(n, 1, "qk", k)
        return put(n + LAG_PARTS, 1, "qk_parts", k)

    for g in range(G):
        hold((g + 1) * block - 1, "max_parts")
        for c in range(2):
            done = g * block + HG * (TH if c == 0 else NST) + 1
            hold(done % slots, "out_copy")
            put_x((done + LAG_OUT) % slots, 0 if done < slots else -1, "out_norm", g, c)
        put_x(g * block + LAG_ROWS, 0 if g < G - 1 else 1, "max_rows", (g + 1) % G)
    for db, g, n in ((0, 3, V_SLOTS[3]), (1, 0, V_SLOTS[0]), (1, 1, V_SLOTS[1]), (1, 2, V_SLOTS[2])):
        put_x(n, db, "v", g, parts=2)
    n = CTX_SLOT
    for hf in range(2):
        for ch in range(C):
            n = put_x(n, -1, "ctx_t", hf, ch)
    for hf in range(2):
        if hf:
            n += LAG_STORE
        put(n, -1, "add_biases", hf)
        n += LAG_BIASES
        for pr in range(2):
            n = put_x(n, -1, "out_proj", hf, pr)
        n = norm(n + 1, -1, 2, hf)
        for ch in range(C):
            n = put_x(n, -1, "x2_t", hf, ch)
        n = put_x(n + 1, -1, "fc1_u", hf)
        for f in range(F):
            while (bank_use[n] or not free(n + 1, "fc1_v.out") or not free(n + 1 + LAG_TANH, "gelu_tanh")
                   or not free(n + 1 + LAG_GELU, "gelu")):
                n += 1
            put_x(n, -1, "fc1_v", hf, f)
            put(n + 2, -1, "gelu_mid", hf, f)
            put(n + 1 + LAG_TANH, -1, "gelu_tanh", hf, f)
            end = put(n + 1 + LAG_GELU, -1, "gelu", hf, f)
            n += GELU_SLOTS
        n = put_x(end + 1, -1, "fc2_u", hf, parts=4)
        for pr in range(2):
            n = put_x(n + 1, -1, "fc2_v", hf, pr)
        put(n + 1, -1 + hf, "load_res", 1 - hf)
        n = norm(n + 1, -1, 3, hf)
        for part in range(5):
            n = put(n, -1, "quant", hf, part) + (LAG_QUANT if part == 3 else 1)
        n += LAG_ZQ
        for ch in range(C):
            n = put_x(n, -1, "zq_t", hf, ch)
        for pr in range(2):
            n = put_x(n + 1, -1, "ffn", hf, pr)
        n = norm(n + LAG_SUM, -1, 4, hf)
        put(n, -1, "store", hf)
    put(0, 1, "load_x", 0)
    put(0, 0, "place", 3)
    n = LN1_SLOT
    for hf in range(2):
        n = norm(n, 1, 1, hf)
        for ch in range(C):
            n = put_x(n, 1, "x1_t", hf, ch)
        if hf == 0:
            put(n, 1, "load_x", 1)
            n += LAG_LOAD
    for k in range(4):
        n = project(n, k)
    assert block <= n + 1 < 2 * block
    put(n + 1, 1, "place", 0)
    put(2 * block, 1, "place", 1)
    n = 2 * block + LAG_PLACE
    for k in range(4, 8):
        n = project(n, k)
    assert n < 3 * block
    put(3 * block, 1, "place", 2)

    out, slot_of = [], []
    for n in range(slots):
        step, hh = divmod(n, HG)
        g, st = divmod(step, NST)
        db, ga = (0, g + 2) if g < 2 else (1, g - 2)
        out += [(0, "scores", (g, st, hh)), (db, "row_max", (ga, st * HG + hh))]
        if n % block == block - 1:
            out.append((db, "max_parts", (ga,)))
        if hh == 1:
            db, m = (0, step - 1) if step else (-1, G * NST - 1)
            out.append((db, "values", divmod(m, NST)))
            c, j = STEPS[m % NST]
            if j == TH * (c + 1) - 1:
                out.append((db, "out_copy", (m // NST, c)))
        out += sorted(more[n], key=lambda entry: not entry[1].startswith("load"))
        if bank_use[n]:
            out.append(bank_use[n])
        slot_of += [n] * (len(out) - len(slot_of))
    return out, slot_of


def last_schedule(schedule, slot_of):
    timed = []
    for (db, stage, a), n in zip(schedule, slot_of):
        base = stage.split(".")[0]
        if db != -1 or (base in AFTER and a[0] == 1):
            continue
        if base == "fc2_u" and not stage.endswith(".out"):
            n += F // 2 - 1 - a[-1]
        use = base in ("out_norm", "ctx_t") + AFTER_BANKS and not stage.endswith(".out")
        timed.append((n, use, 0, (db, stage, a)))
        if base in AFTER:
            timed.append((n + LAST_LAG, use, 1, (db, stage, (1,) + a[1:])))
    timed.append((0, False, 1, (-1, "load_res", (1,))))
    return [entry[3] for entry in sorted(timed, key=lambda e: e[:3])]


def build(nc, hidden, ln1_g, ln1_b, ln2_g, ln2_b, q_U, q_V, q_b, k_U, k_V, k_b, v_U, v_V, v_b,
          out_U, out_V, out_b, fc1_U, fc1_V, fc1_b, fc2_U, fc2_V, fc2_b, ffn_w, in_scale, w_scale,
          ffn_bias, out):
    SCHED, slot_of = schedule()
    LAST = last_schedule(SCHED, slot_of)
    ENTRIES = SCHED + LAST
    with ExitStack() as ctx:
        def sb(name, shape, dt=F32):
            return ctx.enter_context(nc.sbuf_tensor(name, shape, dt))

        def sem(name):
            return ctx.enter_context(nc.semaphore(name))

        slots = sb("slots", [P, G, HG, 2, S], BF16)
        qs, ks = slots[:, :, :, 0, :], slots[:, :, :, 1, :]
        vs = sb("vs", [P, T, H, DH + 1])
        probs = sb("probs", [P, NPT, HG, HALF])
        parts = sb("parts", [P, 2, 3, S], BF16)
        qk_full = sb("qk_full", [P, HALF])
        qk_rest = sb("qk_rest", [P, HALF])
        x_in = sb("x_in", [P, TH, D])
        x1t = sb("x1t", [P, C, S])
        ctx_sb = sb("ctx_sb", [P, T, D])
        ctx_t = sb("ctx_t", [P, 2, C, HALF])
        o_sb = sb("o_sb", [P, HALF])
        x_res = sb("x_res", [P, TH, D])
        h_sb = sb("h_sb", [P, TH, D])
        x2 = sb("x2", [P, TH, D])
        x2t = sb("x2t", [P, C, HALF])
        u_t = sb("u_t", [P, HALF])
        hid = sb("hid", [P, F, HALF])
        w_t = sb("w_t", [P, HALF])
        zq = sb("zq", [P, TH, D], BF16)
        zqt = sb("zqt", [P, C, HALF], BF16)
        yb = sb("yb", [P, TH, D], BF16)
        trash = sb("trash", [P, TRASH, HALF], BF16)
        m_rows = sb("m_rows", [MROWS * HG, S], BF16)
        mx = sb("mx", [P, T, HG])
        mx_hi = sb("mx_hi", [P, TH, HG])
        m_part = sb("m_part", [P, T, HG, MROWS], BF16)
        m_rest = sb("m_rest", [P, T, HG])
        rden = sb("rden", [P, TH, HG, 1])
        LN = range(1, 5)
        st6 = {n: sb(f"st6_{n}", [P, TH, 6]) for n in LN}
        mv = {n: sb(f"mv_{n}", [P, TH, 2]) for n in LN}
        var_eps = {n: sb(f"var_eps_{n}", [P, TH]) for n in LN}
        rstd = {n: sb(f"rstd_{n}", [P, TH]) for n in LN}
        wq = sb("wq", [P, C, D])
        wk = sb("wk", [P, C, D])
        wv = sb("wv", [P, C, D])
        wo = sb("wo", [P, C, D])
        w1u = sb("w1u", [P, C, R_MLP])
        w1v = sb("w1v", [P, FF])
        w2u = sb("w2u", [P, F, R_MLP])
        w2v = sb("w2v", [P, D])
        wf = sb("wf", [P, C, D], BF16)
        vb = sb("vb", [P, 1, H, DH])
        ob = sb("ob", [P, D])
        b2 = sb("b2", [P, D])
        fb = sb("fb", [P, D], BF16)
        g1 = sb("g1", [P, C])
        b1 = sb("b1", [P, C])
        g2 = sb("g2", [P, C])
        bb2 = sb("bb2", [P, C])
        qb = sb("qb", [P, 2])
        kb = sb("kb", [P, 2])
        fc1b = sb("fc1b", [P, F])
        fc1b_sq = sb("fc1b_sq", [P, F])
        sc = sb("sc", [P, 5])
        ident = sb("ident", [P, P])
        ident_b = sb("ident_b", [P, P], BF16)
        mask = sb("mask", [P, HALF])
        mask_t = sb("mask_t", [P, P], BF16)
        half_neg = sb("half_neg", [P, TH])

        bank = [ctx.enter_context(nc.psum_tensor(f"bank{n}", [P, HALF], F32)) for n in range(8)]
        pa, ps, po, px = bank[0:A_RING], bank[A_RING:5], bank[5], bank[6:8]

        names_in = ["q_in", "k_in", "v_in", "out_in", "rest_in"]
        loaded = {n: sem(n) for n in names_in}
        ident_ok, mask_ok, ones_ok = sem("ident_ok"), sem("mask_ok"), sem("ones_ok")
        ut_pe, ut_sb, fold_pe, fold_sb = sem("ut_pe"), sem("ut_sb"), sem("fold_pe"), sem("fold_sb")
        scale_ok, wf_ok, v_zero = sem("scale_ok"), sem("wf_ok"), sem("v_zero")
        x_loaded = sem("x_loaded")
        ln = {n: {k: sem(f"ln{n}_{k}") for k in ("stats", "aggr", "var", "rstd", "norm")} for n in LN}
        x1t_pe, x1t_sb = sem("x1t_pe"), sem("x1t_sb")
        qk_pe, qk_hi, qk_x, qk_r, qk_mid, qk_lo = (sem(n) for n in ("qk_pe", "qk_hi", "qk_x", "qk_r", "qk_mid", "qk_lo"))
        placed = [sem(f"placed{g}") for g in range(G)]
        v_pe, v_sb = sem("v_pe"), sem("v_sb")
        max_scores, row_max, neg_max = sem("max_scores"), sem("row_max"), sem("neg_max")
        mt_pe, mt_sb, m_placed = sem("mt_pe"), sem("mt_sb"), sem("m_placed")
        scores_pe, exp_done, pv_pe = sem("scores_pe"), sem("exp_done"), sem("pv_pe")
        o_copied, o_t, o_rden, ctx_ok = sem("o_copied"), sem("o_t"), sem("o_rden"), sem("ctx_ok")
        res_loaded, res_ob, res_b2, res_h = sem("res_loaded"), sem("res_ob"), sem("res_b2"), sem("res_h")
        ct_pe, ct_sb, op_pe, h_ok = sem("ct_pe"), sem("ct_sb"), sem("op_pe"), sem("h_ok")
        x2t_pe, x2t_sb, u_pe, u_sb = sem("x2t_pe"), sem("x2t_sb"), sem("u_pe"), sem("u_sb")
        hid_pe, hid_raw, hid_sq, hid_mid, hid_tanh, hid_ok = (
            sem(n) for n in ("hid_pe", "hid_raw", "hid_sq", "hid_mid", "hid_tanh", "hid_ok"))
        gelu_ok = sem("gelu_ok")
        w_pe, w_sb, y_pe, y_ok = sem("w_pe"), sem("w_sb"), sem("y_pe"), sem("y_ok")
        quant_v, quant_p = sem("quant_v"), sem("quant_p")
        zt_pe, zt_sb, ffn_pe, ffn_y, ffn_b, ffn_sum = (sem(n) for n in ("zt_pe", "zt_sb", "ffn_pe", "ffn_y", "ffn_b", "ffn_sum"))
        stored = sem("stored")

        raw, tr = (slots[:, 2 * n:2 * n + 2, :, :, :].rearrange("p g h w s -> p (g h w s)").bitcast(F32) for n in range(2))
        u_raw = [raw[:, n * 1536:(n + 1) * 1536].rearrange("p (c x) -> p c x", c=C) for n in range(3)]
        v_raw = [raw[0:2 * R, 4608 + n * D:4608 + (n + 1) * D].rearrange("r (h w e) -> r h w e", w=2, e=DH) for n in range(3)]
        ou_raw = raw[:, 5376:5760].rearrange("p (c x) -> p c x", c=C)
        ov_raw = [raw[:, 5760:6016], raw[0:R_OUT - P, 6016:6272]]
        wf_raw = yb[:, 0:C, :]
        ut = tr[0:2 * R, 0:2048].rearrange("p (h c d) -> p h c d", h=H // 2, c=C)
        out_t = [tr[:, 4096:4352], tr[0:R_OUT - P, 4352:4608]]
        most = {"x_res": x_res, "h_sb": h_sb, "x2": x2, "hid": hid}
        last = {name: raw[:, n * D * TH:n * D * TH + size * w].rearrange("p (t d) -> p t d", t=size)
                for name, n, size, w in (("x_res", 0, TH, D), ("h_sb", 1, TH, D), ("x2", 2, TH, D), ("hid", 3, F, HALF))}
        for m in (most, last):
            for n, name in enumerate(("q_v", "q_m", "q_t", "q_n")):
                m[name] = m["hid"][:, 2 * n:2 * n + 2, :].rearrange("p a b -> p (a b)")

        def is_last(b, hf):
            return isinstance(b, int) and (b, hf) == (B - 1, 1)

        def own(b, hf):
            return last if is_last(b, hf) else most

        squares = [x2t[:, 0, :], x2t[:, 1, :], w_t[:, :]]

        flat = "p a b -> p (a b)"

        def need_first(eng, *events):
            values = [n if isinstance(n, int) else eng.to_reg(n) for _, n in events]
            eng.wait_ge(ident_ok, 4)
            for (s, _), n in zip(events, values):
                need(eng, s, n)

        def need(eng, s, n):
            if not isinstance(n, int) or n > 0:
                eng.wait_ge(s, n)

        def reader(stage, a):
            if stage in ("v", "fc2_u") and a[-1]:
                return None
            return {
                "x1_t": lambda: (x1t_sb, 4, 2 * a[0] + a[1]),
                "qk": lambda: (qk_x, 8, a[0]),
                "v": lambda: (v_sb, 4, a[0]),
                "max_rows": lambda: (mt_sb, 4, a[0]),
                "out_norm": lambda: (ctx_ok, 8, 2 * a[0] + a[1]),
                "ctx_t": lambda: (ct_sb, 4, 2 * a[0] + a[1]),
                "out_proj": lambda: (h_ok, 4, 2 * a[0] + a[1]),
                "x2_t": lambda: (x2t_sb, 4, 2 * a[0] + a[1]),
                "fc1_u": lambda: (u_sb, 2, a[0]),
                "fc1_v": lambda: (hid_sq, 16, F * a[0] + a[1]),
                "fc2_u": lambda: (w_sb, 2, a[0]),
                "fc2_v": lambda: (y_ok, 4, 2 * a[0] + a[1]),
                "zq_t": lambda: (zt_sb, 4, 2 * a[0] + a[1]),
                "ffn": lambda: (ffn_y, 4, 2 * a[0] + a[1]),
            }.get(stage, lambda: None)()

        in_use = [n for n, (_, stage, a) in enumerate(ENTRIES) if reader(stage, a)]
        uses = [n for n in in_use if n < len(SCHED)]
        assert NU == NST * HG and len(uses) % 2 == 0 and all(SCHED[n][0] >= 0 for n in uses[-2:])
        bank_of, using = {}, {}
        for n, (db, stage, a) in enumerate(ENTRIES):
            base = stage.removesuffix(".out")
            kind = (base, a[0]) if base in AFTER else base
            if n in in_use:
                using[kind] = in_use.index(n) % 2
            if reader(base, a) or (base in ("v", "fc2_u")):
                bank_of[n] = using[kind]

        def runs(s, n):
            return not isinstance(s, int) or 0 <= s + ENTRIES[n][0] < B

        def x_read(s, n):
            same = [m for m in uses if bank_of[m] == bank_of[n]]
            before_n = [m for m in in_use if bank_of[m] == bank_of[n] and m < n and (m < len(SCHED)) == (n < len(SCHED))]
            for back, places in ((0, before_n), (1, same), (2, same)):
                before = s - back
                valid = [m for m in places if runs(before, m)]
                if valid:
                    db, stage, a = ENTRIES[valid[-1]]
                    who, per, k = reader(stage, a)
                    return who, (before + db) * per + k + 1
            return None

        def run_steps(eng, stages, between=lambda: None):
            def step(s, entries=range(len(SCHED))):
                for n in entries:
                    db, stage, a = ENTRIES[n]
                    if stage in stages and runs(s, n):
                        if n in bank_of:
                            stages[stage]((s, n), s + db, *a)
                        else:
                            stages[stage](s + db, *a)
            step(-1)
            between()
            step(0)
            step(1)
            with eng.Fori(2, B - 1) as s:
                step(s)
            step(B - 1)
            step(B, range(len(SCHED), len(ENTRIES)))

        def st_width(st):
            c, j = STEPS[st]
            return c, j, max(0, P * (j - TH * c))

        block = ctx.enter_context(nc.Block())

        @block.sync
        def _(sp):
            for name, k, u, v in (("q_in", 0, q_U, q_V), ("k_in", 1, k_U, k_V), ("v_in", 2, v_U, v_V)):
                sp.dma_start(u_raw[k], u.rearrange("(c p) h r -> p c (h r)", p=P)).then_inc(loaded[name], 16)
                if k == 0:
                    sp.wait_ge(v_zero, 1)
                for w in range(2):
                    sp.dma_start(v_raw[k][w * R:(w + 1) * R, :, w, :],
                                 v.rearrange("(h w) r e -> w r h e", w=2)[w]).then_inc(loaded[name], 16)
            sp.dma_start(ou_raw, out_U.rearrange("(c p) r -> p c r", p=P)).then_inc(loaded["out_in"], 16)
            sp.dma_start(ov_raw[0], out_V[0:P, :]).then_inc(loaded["out_in"], 16)
            sp.dma_start(ov_raw[1], out_V[P:R_OUT, :]).then_inc(loaded["out_in"], 16)
            for dst, src in (
                (g1, ln1_g.rearrange("(c p) -> p c", p=P)), (b1, ln1_b.rearrange("(c p) -> p c", p=P)),
                (g2, ln2_g.rearrange("(c p) -> p c", p=P)), (bb2, ln2_b.rearrange("(c p) -> p c", p=P)),
                (qb, q_b.rearrange("(f h) e -> (h e) f", f=2)), (kb, k_b.rearrange("(f h) e -> (h e) f", f=2)),
                (fc1b, fc1_b.rearrange("(f p) -> p f", p=P)),
                (vb[:, 0, :, :], v_b.partition_broadcast(P)),
                (ob, out_b.partition_broadcast(P)), (b2, fc2_b.partition_broadcast(P)),
                (fb, ffn_bias.partition_broadcast(P)),
                (sc[:, 0:1], in_scale.partition_broadcast(P)), (sc[:, 1:2], w_scale.partition_broadcast(P)),
                (w1u, fc1_U.rearrange("(c p) r -> p c r", p=P)), (w1v, fc1_V),
                (w2u, fc2_U.rearrange("(f p) r -> p f r", p=P)), (w2v, fc2_V),
                (wf_raw, ffn_w.rearrange("(c p) n -> p c n", p=P)),
            ):
                with nc.allow_non_contiguous_dma(reason="a few short vectors, one element per partition"):
                    sp.dma_start(dst if isinstance(dst, bass.AP) else dst[:], src).then_inc(loaded["rest_in"], 16)

            def load_x(b, hf):
                need_first(sp, (x1t_pe, b * 4 + 2 * hf))
                sp.dma_start(x_in[:, :, :], hidden[b, hf * HALF:(hf + 1) * HALF, :].rearrange("(t p) d -> p t d", p=P)).then_inc(x_loaded, 16)

            def load_res(b, hf):
                if is_last(b, hf):
                    sp.wait_ge(scores_pe, B * G * NST * HG)
                else:
                    need_first(sp, (y_ok, b * 4 + 2 * hf))
                sp.dma_start(own(b, hf)["x_res"][:, :, :],
                             hidden[b, hf * HALF:(hf + 1) * HALF, :].rearrange("(t p) d -> p t d", p=P)).then_inc(res_loaded, 16)

            def place(b, g):
                done = b * 8 + 4 * (g // 2) + 4
                need_first(sp, (qk_lo, done), (qk_mid, done), (qk_hi, done),
                           (scores_pe, (b - 1) * G * NST * HG + (g + 1) * NST * HG))
                sp.wait_ge(fold_sb, 7)
                both = parts[:, :, :, :].rearrange("p w n s -> p (w n) s")
                for hh in range(HG):
                    lo = (g % 2 * HG + hh) * DH
                    for r in range(SPLIT):
                        qp, kp = Q_PARTS[r], 3 + K_PARTS[r]
                        sp.dma_start(slots[DH * r:DH * (r + 1), g, hh, :, :],
                                     both[lo:lo + DH, qp:kp + 1:kp - qp, :]).then_inc(placed[g], 16)

            def max_rows(xn, b, g):
                need(sp, mt_sb, b * G + g + 1)
                for hh in range(HG):
                    sp.dma_start(qs[KS:KM, g, hh, :], m_rows[MROWS * hh:MROWS * (hh + 1), :]).then_inc(m_placed, 16)

            def store(b, hf):
                need_first(sp, (ln[4]["norm"], b * 8 + 4 * hf + 4))
                sp.dma_start(out[b, hf * HALF:(hf + 1) * HALF, :].rearrange("(t p) d -> p t d", p=P), own(b, hf)["h_sb"][:, :, :]).then_inc(stored, 16)

            run_steps(sp, {"load_x": load_x, "load_res": load_res, "place": place, "max_rows.out": max_rows, "store": store})
            sp.wait_ge(stored, 2 * B * 16)

        @block.gpsimd
        def _(pool):
            pool.memset(raw[0:2 * R, 4608:4608 + 3 * D], 0.0).then_inc(v_zero, 1)
            pool.memset(ident[:, :], 0.0).then_inc(ident_ok, 1)
            pool.memset(ident_b[:, :], 0.0).then_inc(ident_ok, 1)
            pool.wait_ge(ident_ok, 2)
            for m in (ident, ident_b):
                pool.affine_select(out=m[:, :], in_=m[:, :], compare_op=ALU.not_equal, fill=1.0, base=0,
                                   pattern=[[-1, P]], channel_multiplier=1).then_inc(ident_ok, 1)
            pool.memset(mask[:, :], 0.0).then_inc(mask_ok, 1)
            pool.wait_ge(mask_ok, 1)
            pool.affine_select(out=mask[:, HALF - P:HALF], in_=mask[:, HALF - P:HALF], compare_op=ALU.is_ge, fill=NEG,
                               base=0, pattern=[[-1, P]], channel_multiplier=1).then_inc(mask_ok, 1)
            pool.memset(mask_t[:, :], 0.0).then_inc(mask_ok, 1)
            pool.wait_ge(mask_ok, 3)
            pool.affine_select(out=mask_t[:, :], in_=mask_t[:, :], compare_op=ALU.is_ge, fill=NEG,
                               base=0, pattern=[[1, P]], channel_multiplier=-1).then_inc(mask_ok, 1)
            pool.memset(half_neg[:, :], -0.5).then_inc(ones_ok, 1)
            pool.memset(vs[:, :, :, DH:DH + 1], 1.0).then_inc(ones_ok, 1)
            pool.wait_ge(ones_ok, 2)
            def key_ones():
                pool.wait_ge(fold_sb, 7)
                pool.wait_ge(qk_lo, 8)
                pool.memset(ks[KS:KM, :, :, :].bitcast(F32), float(np.uint32(0x3F803F80).view(np.float32))).then_inc(ones_ok, 1)
                pool.wait_ge(ones_ok, 3)

            def power(n):
                def f(b, hf):
                    need(pool, ln[n]["norm"], b * 8 + 4 * hf)
                    need(pool, ln[n]["var"], b * 2 + hf + 1)
                    pool.tensor_tensor(rstd[n][:, :], var_eps[n][:, :], half_neg[:, :], ALU.pow).then_inc(ln[n]["rstd"], 1)
                return f

            def qk(xn, b, n):
                w, hf = n % 4 // 2, n % 2
                cols = slice(hf * HALF, (hf + 1) * HALF)
                need(pool, qk_x, b * 8 + n + 1)
                need(pool, qk_lo, b * 8 + n)
                need(pool, qk_hi, b * 8 + n + 1)
                pool.tensor_tensor(qk_rest[:, :], qk_full[:, :], parts[:, w, 0, cols], ALU.subtract).then_inc(qk_r, 1)

            def qk_parts(b, n):
                w, hf = n % 4 // 2, n % 2
                cols = slice(hf * HALF, (hf + 1) * HALF)
                need(pool, qk_mid, b * 8 + n + 1)
                pool.tensor_tensor(parts[:, w, 2, cols], qk_rest[:, :], parts[:, w, 1, cols], ALU.subtract).then_inc(qk_lo, 1)

            def add_biases(b, hf):
                m = own(b, hf)
                need(pool, res_loaded, (b * 2 + hf + 1) * 16)
                if not is_last(b, hf):
                    need(pool, stored, (b * 2 + hf) * 16)
                need(pool, loaded["rest_in"], 18 * 16)
                for t in range(TH):
                    pool.tensor_tensor(m["h_sb"][:, t, :], m["x_res"][:, t, :], ob[:, :], ALU.add).then_inc(res_ob, 1)
                need(pool, res_ob, (b * 2 + hf + 1) * TH)
                for t in range(TH):
                    pool.tensor_tensor(m["x_res"][:, t, :], m["x_res"][:, t, :], b2[:, :], ALU.add).then_inc(res_b2, 1)

            def fc1_u(xn, b, hf):
                need(pool, h_ok, b * 4 + 2 * hf + 2)
                need(pool, res_b2, (b * 2 + hf + 1) * TH)
                m = own(b, hf)
                xr, hx = m["x_res"][:, :, :].rearrange(flat), m["h_sb"][:, :, :].rearrange(flat)
                pool.tensor_tensor(xr, xr, hx, ALU.add).then_inc(res_h, 1)

            def quant(b, hf, part):
                k = b * 2 + hf
                m = own(b, hf)
                if part < 3:
                    return
                if part == 4:
                    need(pool, quant_v, k * 5 + 5)
                    need(pool, zt_pe, k * C)
                    pool.tensor_tensor(zq[:, :, :].rearrange(flat), m["q_t"], m["q_n"], ALU.add).then_inc(quant_p, 1)
                    return
                need(pool, quant_v, k * 5 + 4)
                pool.tensor_tensor(m["q_t"], m["q_v"], m["q_m"], ALU.add).then_inc(quant_p, 1)
                need(pool, quant_p, k * 3 + 1)
                pool.tensor_tensor(m["q_t"], m["q_t"], m["q_m"], ALU.subtract).then_inc(quant_p, 1)

            def ffn(xn, b, hf, pr):
                k = b * 4 + 2 * hf + pr
                need(pool, ffn_y, k + 1)
                pair = slice(2 * pr, 2 * pr + 2)
                m = own(b, hf)
                for t in (2 * pr, 2 * pr + 1):
                    pool.tensor_tensor(yb[:, t, :], yb[:, t, :], fb[:, :], ALU.add).then_inc(ffn_b, 1)
                need(pool, ffn_b, k * 2 + 2)
                pool.tensor_tensor(m["h_sb"][:, pair, :].rearrange(flat), m["x2"][:, pair, :].rearrange(flat),
                                   yb[:, pair, :].rearrange(flat), ALU.add).then_inc(ffn_sum, 1)

            run_steps(pool, {"ln1_aggr": power(1), "ln2_aggr": power(2), "ln3_aggr": power(3), "ln4_aggr": power(4),
                             "qk.out": qk, "qk_parts": qk_parts, "add_biases": add_biases, "fc1_u.out": fc1_u,
                             "quant": quant, "ffn.out": ffn}, key_ones)

        @block.scalar
        def _(act):
            act.wait_ge(loaded["rest_in"], 18 * 16)

            def x1_t(xn, b, hf, ch):
                need(act, x1t_pe, b * 4 + 2 * hf + ch + 1)
                need(act, v_pe, b * 4)
                need(act, qk_pe, b * 8)
                act.activation(x1t[:, ch, hf * HALF:(hf + 1) * HALF], px[bank_of[xn[1]]][:, :], ACT.Identity,
                               bias=b1[:, ch:ch + 1], scale=g1[:, ch:ch + 1]).then_inc(x1t_sb, 1)

            def qk(xn, b, n):
                f, w, hf = n // 4, n % 4 // 2, n % 2
                cols = slice(hf * HALF, (hf + 1) * HALF)
                bias = (qb, kb)[w][:, f:f + 1]
                need(act, qk_pe, b * 8 + n + 1)
                for g in (0, 1) if f else (2, 3):
                    need(act, placed[g], (b + f) * 16 * HG * SPLIT)
                act.activation(parts[:, w, 0, cols], px[bank_of[xn[1]]][:, :], ACT.Identity, bias=bias).then_inc(qk_hi, 1)
                need(act, qk_r, b * 8 + n)
                act.activation(qk_full[:, :], px[bank_of[xn[1]]][:, :], ACT.Identity, bias=bias).then_inc(qk_x, 1)

            def max_rows(xn, b, g):
                need(act, mt_pe, b * 4 + g + 1)
                need(act, m_placed, (b * 4 + g) * HG * 16)
                act.activation(m_rows[:, :], px[bank_of[xn[1]]][0:MROWS * HG, :].bitcast(BF16), ACT.Copy).then_inc(mt_sb, 1)

            def scores(b, g, st, hh):
                c, j, lo = st_width(st)
                step = g * NST + st
                n = step * HG + hh
                need(act, scores_pe, b * G * NST * HG + n + 1)
                need(act, pv_pe, b * G * NST + step - NPT + 1)
                act.activation(probs[:, step % NPT, hh, lo:HALF], ps[n % S_RING][:, lo:HALF], ACT.Exp,
                               scale=SCALE).then_inc(exp_done, 1)

            def out_copy(b, g, c):
                k = 2 * g + c
                need(act, pv_pe, b * G * NST + g * NST + (NST if c else TH))
                need(act, o_t, b * 8 + k)
                act.activation(o_sb[:, :], po[:, :], ACT.Copy).then_inc(o_copied, 1)

            def ctx_tr(xn, b, hf, ch):
                need(act, ct_pe, b * 4 + 2 * hf + ch + 1)
                need(act, op_pe, b * 4)
                act.activation(ctx_t[:, hf, ch, :], px[bank_of[xn[1]]][:, :], ACT.Copy).then_inc(ct_sb, 1)

            def x2_t(xn, b, hf, ch):
                need(act, x2t_pe, b * 4 + 2 * hf + ch + 1)
                need(act, hid_ok, (b * 2 + hf) * F)
                act.activation(x2t[:, ch, :], px[bank_of[xn[1]]][:, :], ACT.Identity,
                               bias=bb2[:, ch:ch + 1], scale=g2[:, ch:ch + 1]).then_inc(x2t_sb, 1)

            def fc1_u(xn, b, hf):
                need(act, u_pe, b * 2 + hf + 1)
                need(act, hid_pe, (b * 2 + hf) * F)
                act.activation(u_t[:, :], px[bank_of[xn[1]]][:, :], ACT.Copy).then_inc(u_sb, 1)

            def fc1_v(xn, b, hf, f):
                k = (b * 2 + hf) * F + f
                x = px[bank_of[xn[1]]][:, :]
                need(act, hid_pe, k + 1)
                if not is_last(b, hf):
                    need(act, w_pe, b * 2 + hf)
                    need(act, quant_p, (b * 2 + hf) * 3)
                act.activation(own(b, hf)["hid"][:, f, :], x, ACT.Identity, bias=fc1b[:, f:f + 1]).then_inc(hid_raw, 1)
                need(act, hid_ok, k - 2)
                if f == 2:
                    need(act, y_pe, (b * 2 + hf) * 2)
                act.wait_ge(gelu_ok, 1)
                act.activation(squares[f % 3], x, ACT.Square, bias=fc1b_sq[:, f:f + 1],
                               scale=GELU_3 ** 0.5).then_inc(hid_sq, 1)

            def gelu_tanh(b, hf, f):
                need(act, hid_mid, (b * 2 + hf) * F + f + 1)
                act.activation(squares[f % 3], squares[f % 3], ACT.Tanh).then_inc(hid_tanh, 1)

            def fc2_u(xn, b, hf):
                need(act, w_pe, b * 2 + hf + 1)
                need(act, y_pe, (b * 2 + hf) * 2)
                act.activation(w_t[:, :], px[bank_of[xn[1]]][:, :], ACT.Copy).then_inc(w_sb, 1)

            def zq_t(xn, b, hf, ch):
                need(act, zt_pe, b * 4 + 2 * hf + ch + 1)
                need(act, ffn_pe, (b * 2 + hf) * 2)
                act.activation(zqt[:, ch, :], px[bank_of[xn[1]]][:, 0:HALF // 2].bitcast(BF16), ACT.Copy).then_inc(zt_sb, 1)

            def ffn(xn, b, hf, pr):
                k = b * 4 + 2 * hf + pr
                need(act, ffn_pe, k + 1)
                act.wait_ge(scale_ok, 3)
                act.activation(yb[:, 2 * pr:2 * pr + 2, :].rearrange(flat), px[bank_of[xn[1]]][:, :], ACT.Copy,
                               scale=sc[:, 4:5]).then_inc(ffn_y, 1)

            run_steps(act, {"x1_t.out": x1_t, "qk.out": qk, "max_rows.out": max_rows, "scores": scores,
                            "out_copy": out_copy, "ctx_t.out": ctx_tr, "x2_t.out": x2_t, "fc1_u.out": fc1_u,
                            "fc1_v.out": fc1_v, "gelu_tanh": gelu_tanh, "fc2_u.out": fc2_u, "zq_t.out": zq_t, "ffn.out": ffn})

        @block.tensor
        def _(pe):
            pe.wait_ge(ident_ok, 4)
            for w, name in enumerate(("q_in", "k_in", "v_in")):
                pe.wait_ge(loaded[name], 48)
                for h4 in range(H // 4):
                    n = w * (H // 4) + h4
                    if n >= 4:
                        pe.wait_ge(ut_sb, n - 3)
                    for hl in range(2):
                        for c in range(C):
                            k = 2 * hl + c
                            last = pe.transpose(bank[n % 4][0:2 * R, k * P:(k + 1) * P],
                                                u_raw[w][:, c, (4 * h4 + 2 * hl) * R:(4 * h4 + 2 * hl + 2) * R], ident[:, :])
                    last.then_inc(ut_pe, 1)
                pe.wait_ge(ut_sb, (w + 1) * (H // 4))
                if w >= 2:
                    pe.wait_ge(fold_sb, w - 1)
                for c in range(C):
                    for h2 in range(H // 2):
                        last = pe.matmul(bank[4 + w % 2][:, c * D + h2 * 2 * DH:c * D + (h2 + 1) * 2 * DH], ut[:, h2, c, :],
                                         v_raw[w][:, h2, :, :].rearrange("r w e -> r (w e)"), start=True, stop=True)
                last.then_inc(fold_pe, 1)
            pe.wait_ge(loaded["out_in"], 48)
            for c in range(C):
                pe.transpose(bank[6][:, c * P:(c + 1) * P], ou_raw[:, c, 0:P], ident[:, :])
                last = pe.transpose(bank[7][0:R_OUT - P, c * P:(c + 1) * P], ou_raw[:, c, P:R_OUT], ident[:, :])
            last.then_inc(fold_pe, 1)
            pe.wait_ge(fold_sb, 5)
            for c in range(C):
                pe.matmul(bank[5][:, c * D:(c + 1) * D], out_t[0][:, c * P:(c + 1) * P], ov_raw[0], start=True, stop=False)
                last = pe.matmul(bank[5][:, c * D:(c + 1) * D], out_t[1][:, c * P:(c + 1) * P], ov_raw[1], start=False, stop=True)
            last.then_inc(fold_pe, 1)
            pe.wait_ge(fold_sb, 6)
            pe.wait_ge(loaded["rest_in"], 18 * 16)
            pe.wait_ge(mask_ok, 4)

            def x_bank(xn):
                free = x_read(*xn)
                if free:
                    need(pe, *free)
                return px[bank_of[xn[1]]]

            def turn(x, src, s, idn):
                for t in range(TH):
                    last = pe.transpose(x[:, t * P:(t + 1) * P], src(t), idn[:, :])
                last.then_inc(s, 1)

            def x1_t(xn, b, hf, ch):
                x = x_bank(xn)
                need(pe, ln[1]["norm"], b * 8 + 4 * hf + 4)
                turn(x, lambda t: x_in[:, t, ch * P:(ch + 1) * P], x1t_pe, ident)

            def qk(xn, b, n):
                x = x_bank(xn)
                f, w, hf = n // 4, n % 4 // 2, n % 2
                need(pe, x1t_sb, b * 4 + 2 * hf + 2)
                for ch in range(C):
                    last = pe.matmul(x[:, :], (wq, wk)[w][:, ch, f * P:(f + 1) * P], x1t[:, ch, hf * HALF:(hf + 1) * HALF],
                                     start=(ch == 0), stop=(ch == C - 1))
                last.then_inc(qk_pe, 1)

            def v(xn, b, g, part):
                x = px[bank_of[xn[1]]] if part else x_bank(xn)
                need(pe, x1t_sb, b * 4 + 4)
                gd = HG * DH
                for t in range(TH * part, TH * (part + 1)):
                    for ch in range(C):
                        last = pe.matmul(x[:, t * gd:(t + 1) * gd], x1t[:, ch, t * P:(t + 1) * P],
                                         wv[:, ch, g * gd:(g + 1) * gd], start=(ch == 0), stop=(ch == C - 1))
                if part:
                    last.then_inc(v_pe, 1)

            def row_max_(b, g, u):
                hh, i, part = UNITS[u]
                n = g * NU + u
                if u == 0:
                    need(pe, placed[g], (b + 1) * 16 * HG * SPLIT)
                need(pe, row_max, b * G * NU + n - A_RING + 1)
                k1 = min((i + 1) * P, (part + 1) * HALF)
                pe.matmul(pa[n % A_RING][:, 0:k1 - part * HALF], qs[0:KS, g, hh, i * P:(i + 1) * P],
                          ks[0:KS, g, hh, part * HALF:k1], start=True, stop=True).then_inc(max_scores, 1)

            def max_rows(xn, b, g):
                x = x_bank(xn)[0:MROWS * HG, :].bitcast(BF16)
                need(pe, neg_max, (b * 4 + g + 1) * 5)
                for i in range(T):
                    last = pe.transpose(x[:, i * P:(i + 1) * P], m_part[:, i, :, :].rearrange(flat), ident_b[:, :])
                last.then_inc(mt_pe, 1)

            def scores(b, g, st, hh):
                c, j, lo = st_width(st)
                n = (g * NST + st) * HG + hh
                if st == 0 and hh == 0:
                    pe.wait_ge(ones_ok, 3)
                    need(pe, m_placed, (b * 4 + g + 1) * HG * 16)
                need(pe, exp_done, b * G * NST * HG + n - S_RING + 1)
                last = pe.matmul(ps[n % S_RING][:, lo:HALF], ks[0:KM, g, hh, j * P:(j + 1) * P],
                                 qs[0:KM, g, hh, c * HALF + lo:(c + 1) * HALF], start=True, stop=st not in DIAG)
                if st in DIAG:
                    last = pe.matmul(ps[n % S_RING][:, lo:lo + P], ident_b[:, :], mask_t[:, :], start=False, stop=True)
                last.then_inc(scores_pe, 1)

            def values(b, g, st):
                c, j, lo = st_width(st)
                step = g * NST + st
                if st == 0:
                    need(pe, v_sb, b * 4 + g + 1)
                if j == 0:
                    need(pe, o_copied, b * 8 + 2 * g + c)
                need(pe, exp_done, (b * G * NST + step) * HG + HG)
                for hh in range(HG):
                    last = pe.matmul(po[32 * hh:32 * hh + DH + 1, lo:HALF], vs[:, j, g * HG + hh, :],
                                     probs[:, step % NPT, hh, lo:HALF], start=(j == 0), stop=(j == TH * (c + 1) - 1))
                last.then_inc(pv_pe, 1)

            def out_norm(xn, b, g, c):
                x = x_bank(xn)
                need(pe, o_copied, b * 8 + 2 * g + c + 1)
                turn(x, lambda t: o_sb[:, t * P:(t + 1) * P], o_t, ident)

            def ctx_tr(xn, b, hf, ch):
                x = x_bank(xn)
                need(pe, ctx_ok, b * 8 + 2 * (G - 1) + hf + 1)
                turn(x, lambda t: ctx_sb[:, TH * hf + t, ch * P:(ch + 1) * P], ct_pe, ident)

            def out_proj(xn, b, hf, pr):
                x = x_bank(xn)
                need(pe, ct_sb, b * 4 + 2 * hf + 2)
                for tt in range(2):
                    for ch in range(C):
                        t = 2 * pr + tt
                        last = pe.matmul(x[:, tt * D:(tt + 1) * D], ctx_t[:, hf, ch, t * P:(t + 1) * P], wo[:, ch, :],
                                         start=(ch == 0), stop=(ch == C - 1))
                last.then_inc(op_pe, 1)

            def x2_t(xn, b, hf, ch):
                x = x_bank(xn)
                need(pe, ln[2]["norm"], b * 8 + 4 * hf + 4)
                turn(x, lambda t: own(b, hf)["x2"][:, t, ch * P:(ch + 1) * P], x2t_pe, ident)

            def fc1_u(xn, b, hf):
                x = x_bank(xn)
                need(pe, x2t_sb, b * 4 + 2 * hf + 2)
                for ch in range(C):
                    last = pe.matmul(x[:, :], w1u[:, ch, :], x2t[:, ch, :], start=(ch == 0), stop=(ch == C - 1))
                last.then_inc(u_pe, 1)

            def fc1_v(xn, b, hf, f):
                x = x_bank(xn)
                need(pe, u_sb, b * 2 + hf + 1)
                pe.matmul(x[:, :], w1v[:, f * P:(f + 1) * P], u_t[:, :], start=True, stop=True).then_inc(hid_pe, 1)

            def fc2_u(xn, b, hf, part):
                x = px[bank_of[xn[1]]] if part else x_bank(xn)
                need(pe, gelu_ok, 2)
                need(pe, hid_ok, (b * 2 + hf + 1) * F)
                for f in range(2 * part, 2 * part + 2):
                    last = pe.matmul(x[:, :], w2u[:, f, :], own(b, hf)["hid"][:, f, :], start=(f == 0), stop=(f == F - 1))
                if part == F // 2 - 1:
                    last.then_inc(w_pe, 1)

            def fc2_v(xn, b, hf, pr):
                x = x_bank(xn)
                need(pe, w_sb, b * 2 + hf + 1)
                for tt in range(2):
                    t = 2 * pr + tt
                    last = pe.matmul(x[:, tt * D:(tt + 1) * D], w_t[:, t * P:(t + 1) * P], w2v[:, :], start=True, stop=True)
                last.then_inc(y_pe, 1)

            def zq_t(xn, b, hf, ch):
                x = x_bank(xn)[:, 0:HALF // 2].bitcast(BF16)
                need(pe, quant_p, (b * 2 + hf + 1) * 3)
                turn(x, lambda t: zq[:, t, ch * P:(ch + 1) * P], zt_pe, ident_b)

            def ffn(xn, b, hf, pr):
                x = x_bank(xn)
                pe.wait_ge(wf_ok, 7)
                need(pe, zt_sb, b * 4 + 2 * hf + 2)
                for tt in range(2):
                    t = 2 * pr + tt
                    for ch in range(C):
                        last = pe.matmul(x[:, tt * D:(tt + 1) * D], zqt[:, ch, t * P:(t + 1) * P], wf[:, ch, :],
                                         start=(ch == 0), stop=(ch == C - 1))
                last.then_inc(ffn_pe, 1)

            run_steps(pe, {"x1_t": x1_t, "qk": qk, "v": v, "row_max": row_max_, "max_rows": max_rows, "scores": scores,
                           "values": values, "out_norm": out_norm, "ctx_t": ctx_tr, "out_proj": out_proj, "x2_t": x2_t,
                           "fc1_u": fc1_u, "fc1_v": fc1_v, "fc2_u": fc2_u, "fc2_v": fc2_v, "zq_t": zq_t, "ffn": ffn})

        @block.vector
        def _(dve):
            dve.memset(po[:, :], 0.0).then_inc(fold_sb, 1)
            for w in range(3):
                for h4 in range(H // 4):
                    n = w * (H // 4) + h4
                    dve.wait_ge(ut_pe, n + 1)
                    if h4 == 0 and w:
                        dve.wait_ge(fold_pe, w)
                    dve.tensor_copy(ut[:, 2 * h4:2 * h4 + 2, :, :].rearrange("p h c d -> p (h c d)"),
                                    bank[n % 4][0:2 * R, :]).then_inc(ut_sb, 1)
                dve.wait_ge(fold_pe, w + 1)
                dve.tensor_copy((wq, wk, wv)[w][:, :, :].rearrange(flat), bank[4 + w % 2][:, :]).then_inc(fold_sb, 1)
            dve.wait_ge(fold_pe, 4)
            dve.tensor_copy(out_t[0], bank[6][:, 0:D])
            dve.tensor_copy(out_t[1], bank[7][0:R_OUT - P, 0:D]).then_inc(fold_sb, 1)
            dve.wait_ge(fold_pe, 5)
            dve.tensor_copy(wo[:, :, :].rearrange(flat), bank[5][:, :]).then_inc(fold_sb, 1)
            dve.wait_ge(fold_sb, 6)
            dve.memset(po[:, :], 0.0).then_inc(fold_sb, 1)
            dve.wait_ge(loaded["rest_in"], 18 * 16)

            def set_up_rest():
                dve.tensor_scalar(fc1b_sq[:, :], fc1b[:, :], GELU_3 ** 0.5, None, ALU.mult).then_inc(gelu_ok, 1)
                dve.tensor_scalar(w2u[:, :, :].rearrange(flat), w2u[:, :, :].rearrange(flat), 0.5, None, ALU.mult).then_inc(gelu_ok, 1)
                dve.reciprocal(sc[:, 2:3], sc[:, 0:1]).then_inc(scale_ok, 1)
                dve.reciprocal(sc[:, 3:4], sc[:, 1:2]).then_inc(scale_ok, 1)
                dve.tensor_tensor(sc[:, 4:5], sc[:, 0:1], sc[:, 1:2], ALU.mult).then_inc(scale_ok, 1)
                dve.wait_ge(scale_ok, 3)
                wv_, wm, wt, wn = (a[:, 0:C * D] for a in (most["q_v"], most["q_m"], most["q_t"], most["q_n"]))
                dve.tensor_scalar(wv_, wf_raw[:, :, :].rearrange(flat), sc[:, 3:4], None, ALU.mult).then_inc(wf_ok, 1)
                dve.wait_ge(wf_ok, 1)
                dve.tensor_scalar(wm.bitcast(U32), wv_.bitcast(U32), 0x7F800000, None, ALU.bitwise_and).then_inc(wf_ok, 1)
                dve.wait_ge(wf_ok, 2)
                dve.tensor_scalar(wm, wm, 2.0 ** -6, 1.5 * 2.0 ** 20, ALU.max, ALU.mult).then_inc(wf_ok, 1)
                dve.wait_ge(wf_ok, 3)
                dve.tensor_tensor(wt, wv_, wm, ALU.add).then_inc(wf_ok, 1)
                dve.wait_ge(wf_ok, 4)
                dve.tensor_tensor(wt, wt, wm, ALU.subtract).then_inc(wf_ok, 1)
                dve.wait_ge(wf_ok, 5)
                dve.tensor_scalar(wn, wt, 7.4e35, 0.0, ALU.mult, ALU.mult).then_inc(wf_ok, 1)
                dve.wait_ge(wf_ok, 6)
                dve.tensor_tensor(wf[:, :, :].rearrange(flat), wt, wn, ALU.add).then_inc(wf_ok, 1)

            def buffer(name, b, hf):
                return x_in if name == "x_in" else own(b, hf)[name]

            def stats(n, buf, ready):
                def f(b, hf, t0):
                    k = b * 2 + hf
                    if t0 == 0:
                        need(dve, *ready(b, hf))
                        need(dve, ln[n]["aggr"], k * TH)
                    for t in (t0, t0 + 1):
                        dve.bn_stats(st6[n][:, t, :], buffer(buf, b, hf)[:, t, :]).then_inc(ln[n]["stats"], 1)
                return f

            def aggr(n):
                def f(b, hf):
                    s = ln[n]
                    k = b * 2 + hf
                    need_first(dve, (s["stats"], (k + 1) * TH), (s["norm"], k * TH), (s["var"], k))
                    for t in range(TH):
                        dve.bn_aggr(mv[n][:, t, :], st6[n][:, t, :]).then_inc(s["aggr"], 1)
                    need(dve, s["aggr"], (k + 1) * TH)
                    need(dve, s["rstd"], k)
                    dve.tensor_scalar(var_eps[n][:, :], mv[n][:, :, 1], EPS, None, ALU.add).then_inc(s["var"], 1)
                return f

            def apply(n, src, dst, free):
                def f(b, hf, t0):
                    s = ln[n]
                    if t0 == 0:
                        need(dve, s["rstd"], b * 2 + hf + 1)
                        if free and not (n == 2 and is_last(b, hf)):
                            need(dve, *free(b, hf))
                    for t in (t0, t0 + 1):
                        dve.tensor_scalar(buffer(dst, b, hf)[:, t, :], buffer(src, b, hf)[:, t, :], mv[n][:, t, 0:1], rstd[n][:, t:t + 1],
                                          ALU.subtract, ALU.mult).then_inc(s["norm"], 1)
                return f

            def qk_parts(b, n):
                w, hf = n % 4 // 2, n % 2
                need(dve, qk_r, b * 8 + n + 1)
                dve.tensor_copy(parts[:, w, 1, hf * HALF:(hf + 1) * HALF], qk_rest[:, :]).then_inc(qk_mid, 1)

            def v(xn, b, g):
                need(dve, v_pe, b * 4 + g + 1)
                need(dve, pv_pe, (b - 1) * G * NST + (g + 1) * NST)
                heads = slice(g * HG, (g + 1) * HG)
                dve.tensor_tensor(vs[:, :, heads, 0:DH], px[bank_of[xn[1]]][:, :].rearrange("p (t h e) -> p t h e", t=T, h=HG),
                                  vb[:, :, heads, :].to_broadcast([P, T, HG, DH]), ALU.add).then_inc(v_sb, 1)

            def row_max_(b, g, u):
                hh, i, part = UNITS[u]
                n = g * NU + u
                k = b * G * NU + n
                if u == 0:
                    need(dve, neg_max, (b * 4 + g) * 5)
                need(dve, row_max, k - TRASH + 1)
                need_first(dve, (max_scores, k + 1))
                dst = (mx_hi[:, i - TH, hh:hh + 1] if part else mx[:, i, hh:hh + 1])
                if i >= TH and part == 0:
                    dve.tensor_reduce(dst, pa[n % A_RING][:, :], AX.X, ALU.max).then_inc(row_max, 1)
                else:
                    w = (i + 1) * P - part * HALF
                    dve.tensor_tensor_reduce(trash[:, n % TRASH, 0:w], pa[n % A_RING][:, 0:w], mask[:, HALF - w:HALF],
                                             1.0, 3.0 * NEG, ALU.add, ALU.max, dst).then_inc(row_max, 1)

            def max_parts(b, g):
                k = (b * 4 + g) * 5
                need(dve, row_max, (b * G + g + 1) * NU)
                dve.tensor_tensor(mx[:, TH:T, :], mx[:, TH:T, :], mx_hi[:, :, :], ALU.max).then_inc(neg_max, 1)
                need(dve, neg_max, k + 1)
                need(dve, mt_pe, b * 4 + g)
                dve.tensor_scalar(m_part[:, :, :, 0], mx[:, :, :], -1.0, None, ALU.mult).then_inc(neg_max, 1)
                need(dve, neg_max, k + 2)
                dve.scalar_tensor_tensor(out=m_rest[:, :, :], in0=mx[:, :, :], scalar=-1.0, in1=m_part[:, :, :, 0],
                                         op0=ALU.mult, op1=ALU.subtract).then_inc(neg_max, 1)
                need(dve, neg_max, k + 3)
                dve.tensor_copy(m_part[:, :, :, 1], m_rest[:, :, :]).then_inc(neg_max, 1)
                need(dve, neg_max, k + 4)
                dve.tensor_tensor(m_part[:, :, :, 2], m_rest[:, :, :], m_part[:, :, :, 1], ALU.subtract).then_inc(neg_max, 1)

            def out_norm(xn, b, g, c):
                k = b * 8 + 2 * g + c
                x = px[bank_of[xn[1]]][:, :].rearrange("p (t h e) -> p t h e", t=TH, h=HG)
                need(dve, o_t, k + 1)
                need(dve, ctx_ok, k)
                dve.reciprocal(rden[:, :, :, :], x[:, :, :, DH:DH + 1]).then_inc(o_rden, 1)
                need(dve, o_rden, k + 1)
                need(dve, ct_pe, (b - 1) * 4 + 2 * c + 2)
                dst = ctx_sb[:, TH * c:TH * (c + 1), g * HG * DH:(g + 1) * HG * DH].rearrange("p t (h e) -> p t h e", h=HG)
                dve.tensor_tensor(dst, x[:, :, :, 0:DH], rden[:, :, :, :].to_broadcast([P, TH, HG, DH]),
                                  ALU.mult).then_inc(ctx_ok, 1)

            def out_proj(xn, b, hf, pr):
                k = b * 4 + 2 * hf + pr
                need(dve, op_pe, k + 1)
                need(dve, res_ob, (b * 2 + hf + 1) * TH)
                dst = own(b, hf)["h_sb"][:, 2 * pr:2 * pr + 2, :].rearrange(flat)
                dve.tensor_tensor(dst, px[bank_of[xn[1]]][:, :], dst, ALU.add).then_inc(h_ok, 1)

            def gelu_mid(b, hf, f):
                k = (b * 2 + hf) * F + f
                need(dve, hid_sq, k + 1)
                need(dve, hid_raw, k + 1)
                dve.scalar_tensor_tensor(out=squares[f % 3], in0=squares[f % 3], scalar=GELU_1, in1=own(b, hf)["hid"][:, f, :],
                                         op0=ALU.add, op1=ALU.mult).then_inc(hid_mid, 1)

            def gelu(b, hf, f):
                need(dve, hid_tanh, (b * 2 + hf) * F + f + 1)
                dve.scalar_tensor_tensor(out=own(b, hf)["hid"][:, f, :], in0=squares[f % 3], scalar=1.0, in1=own(b, hf)["hid"][:, f, :],
                                         op0=ALU.add, op1=ALU.mult).then_inc(hid_ok, 1)

            def fc2_v(xn, b, hf, pr):
                need(dve, y_pe, b * 4 + 2 * hf + pr + 1)
                need(dve, res_h, b * 2 + hf + 1)
                pair = slice(2 * pr, 2 * pr + 2)
                dve.tensor_tensor(own(b, hf)["h_sb"][:, pair, :].rearrange(flat), px[bank_of[xn[1]]][:, :],
                                  own(b, hf)["x_res"][:, pair, :].rearrange(flat), ALU.add).then_inc(y_ok, 1)

            def quant(b, hf, part):
                k = (b * 2 + hf) * 5
                m = own(b, hf)
                z16 = yb[:, :, :].rearrange(flat)
                if part == 0:
                    need(dve, ln[3]["norm"], (b * 2 + hf + 1) * TH)
                    need(dve, ffn_sum, (b * 2 + hf) * 2)
                    dve.tensor_copy(z16, m["x2"][:, :, :].rearrange(flat)).then_inc(quant_v, 1)
                elif part == 1:
                    need(dve, w_pe, b * 2 + hf + 1)
                    need(dve, quant_v, k + 1)
                    dve.tensor_scalar(m["q_v"], z16, sc[:, 2:3], None, ALU.mult).then_inc(quant_v, 1)
                elif part == 2:
                    need(dve, quant_v, k + 2)
                    dve.tensor_scalar(m["q_m"].bitcast(U32), m["q_v"].bitcast(U32), 0x7F800000, None, ALU.bitwise_and).then_inc(quant_v, 1)
                elif part == 3:
                    need(dve, quant_v, k + 3)
                    dve.tensor_scalar(m["q_m"], m["q_m"], 2.0 ** -6, 1.5 * 2.0 ** 20, ALU.max, ALU.mult).then_inc(quant_v, 1)
                else:
                    need(dve, quant_p, (b * 2 + hf) * 3 + 2)
                    dve.tensor_scalar(m["q_n"], m["q_t"], 7.4e35, 0.0, ALU.mult, ALU.mult).then_inc(quant_v, 1)

            run_steps(dve, {
                "ln1_stats": stats(1, "x_in", lambda b, hf: (x_loaded, (b * 2 + hf + 1) * 16)),
                "ln1_aggr": aggr(1),
                "ln1_apply": apply(1, "x_in", "x_in", None),
                "ln2_stats": stats(2, "h_sb", lambda b, hf: (h_ok, b * 4 + 2 * hf + 2)),
                "ln2_aggr": aggr(2),
                "ln2_apply": apply(2, "h_sb", "x2", lambda b, hf: (ffn_sum, (b * 2 + hf) * 2)),
                "ln3_stats": stats(3, "h_sb", lambda b, hf: (y_ok, b * 4 + 2 * hf + 2)),
                "ln3_aggr": aggr(3),
                "ln3_apply": apply(3, "h_sb", "x2", lambda b, hf: (x2t_pe, b * 4 + 2 * hf + 2)),
                "ln4_stats": stats(4, "h_sb", lambda b, hf: (ffn_sum, b * 4 + 2 * hf + 2)),
                "ln4_aggr": aggr(4),
                "ln4_apply": apply(4, "h_sb", "h_sb", None),
                "qk_parts": qk_parts, "v.out": v, "row_max": row_max_, "max_parts": max_parts,
                "out_norm.out": out_norm, "out_proj.out": out_proj, "gelu_mid": gelu_mid, "gelu": gelu,
                "fc2_v.out": fc2_v, "quant": quant}, set_up_rest)


_INS = ["L0_attn_hidden_states", "L0_attn_ln1_g", "L0_attn_ln1_b", "L0_attn_ln2_g", "L0_attn_ln2_b",
        "L0_attn_q_U", "L0_attn_q_V", "L0_attn_q_b", "L0_attn_k_U", "L0_attn_k_V", "L0_attn_k_b",
        "L0_attn_v_U", "L0_attn_v_V", "L0_attn_v_b", "L0_attn_out_U", "L0_attn_out_V", "L0_attn_out_b",
        "L0_attn_fc1_U", "L0_attn_fc1_V", "L0_attn_fc1_b", "L0_attn_fc2_U", "L0_attn_fc2_V", "L0_attn_fc2_b",
        "L0_ffn_kernel", "L0_ffn_input_scale", "L0_ffn_kernel_scale", "L0_ffn_bias"]


def kernel(**inputs):
    import numpy as _np
    import concourse.bacc as _bacc
    from concourse import mybir as _mybir
    from concourse.bass_utils import run_bass_kernel_spmd as _run

    nc = _bacc.Bacc("TRN2", target_bir_lowering=False, num_devices=1)
    arrays, args = {}, []
    for name in _INS:
        a = _np.ascontiguousarray(inputs[name])
        arrays[f"in_{name}"] = a
        args.append(nc.dram_tensor(f"in_{name}", a.shape, _mybir.dt.from_np(a.dtype), kind="ExternalInput").ap())
    args.append(nc.dram_tensor("out_0", (B, S, D), _mybir.dt.float32, kind="ExternalOutput").ap())
    build(nc, *args)
    r = _run(nc, [arrays], core_ids=[0])
    return r.results[0]["out_0"]
```
